# Optimizing a Trainium2 kernel written in Bass

```python
import numpy as np
import jax
import jax.numpy as jnp

def _softmax(x, axis=-1):
    return jax.nn.softmax(x, axis=axis)

def _gelu(x):
    return jax.nn.gelu(x, approximate=True)

def _silu(x):
    return jax.nn.silu(x)

def _sigmoid(x):
    return jax.nn.sigmoid(x)

def _layernorm(x, axis=-1, eps=1e-05):
    m = jnp.mean(x, axis=axis, keepdims=True)
    v = jnp.var(x, axis=axis, keepdims=True)
    return (x - m) / jnp.sqrt(v + eps)

def _scatter_add(tgt, idx, src, axis=0):
    return tgt.at[idx].add(src)

def _segment_sum(src, seg, n):
    return jax.ops.segment_sum(src, seg, n)
kernel_name = 'mk_prb_d1_jaxref_r4_3da668'

def setup_inputs(seed: int=0):
    np.random.seed(seed)
    _w = jnp.asarray

    def _L0_attn_setup():
        import jax, jax.numpy as jnp
        import numpy as np
        DIM = 256
        HEADS = 16
        DIM_HEAD = 64
        WINDOW = 64
        NEG = -1000000000.0

        def rms_norm(x, gamma, size):
            nrm = jnp.sqrt(jnp.sum(x * x, axis=-1, keepdims=True))
            return x / jnp.maximum(nrm, 1e-12) * size ** 0.5 * gamma

        def sliding_window_attention(q, k, v, window):
            b, h, S, d = q.shape
            Bk = window
            nb = S // Bk
            qb = q.reshape(b, h, nb, Bk, d)
            kb = k.reshape(b, h, nb, Bk, d)
            vb = v.reshape(b, h, nb, Bk, d)
            k_prev = jnp.pad(kb, ((0, 0), (0, 0), (1, 0), (0, 0), (0, 0)))[:, :, :nb]
            v_prev = jnp.pad(vb, ((0, 0), (0, 0), (1, 0), (0, 0), (0, 0)))[:, :, :nb]
            kctx = jnp.concatenate([k_prev, kb], axis=3)
            vctx = jnp.concatenate([v_prev, vb], axis=3)
            scale = 1.0 / jnp.sqrt(jnp.asarray(d, q.dtype))
            scores = jnp.einsum('bhnqd,bhnkd->bhnqk', qb, kctx) * scale
            qi = jnp.arange(Bk)[:, None]
            kj = jnp.arange(2 * Bk)[None, :]
            diff = Bk + qi - kj
            base = (diff >= 0) & (diff <= window)
            blk = jnp.arange(nb)[:, None, None]
            key_exists = (blk - 1) * Bk + kj[None] >= 0
            mask = base[None] & key_exists
            scores = jnp.where(mask[None, None], scores, NEG)
            attn = jax.nn.softmax(scores, axis=-1)
            out = jnp.einsum('bhnqk,bhnkd->bhnqd', attn, vctx)
            return out.reshape(b, h, S, d)
        key = jax.random.key(seed)
        ks = jax.random.split(key, 6)
        b, S = (2, 1024)
        dim_inner = HEADS * DIM_HEAD
        x = jax.random.normal(ks[0], (b, S, DIM), dtype=jnp.float32)
        gamma = jnp.ones((DIM,), dtype=jnp.float32)
        W_qkv = jax.random.normal(ks[1], (DIM, 3 * dim_inner), dtype=jnp.float32) * 0.02
        W_gates = jax.random.normal(ks[2], (DIM, HEADS), dtype=jnp.float32) * 0.02
        b_gates = jnp.zeros((HEADS,), dtype=jnp.float32)
        W_out = jax.random.normal(ks[3], (dim_inner, DIM), dtype=jnp.float32) * 0.02
        return {'x': x, 'gamma': gamma, 'W_qkv': W_qkv, 'W_gates': W_gates, 'b_gates': b_gates, 'W_out': W_out}
    _L0_attn_in = _L0_attn_setup()

    def _L0_ffn_setup():
        import jax, jax.numpy as jnp
        import numpy as np
        DIM = 256
        DEPTH = 2
        HEADS = 8
        DIM_HEAD = 64
        WINDOW = 128
        INNER = HEADS * DIM_HEAD
        HID = int(DIM * 4 * 2 / 3)
        B, N = (2, 2048)
        QK_SCALE = 8.0

        def shift_token(t):
            t1, t2 = jnp.split(t, 2, axis=-1)
            t2 = jnp.pad(t2, ((0, 0), (1, 0), (0, 0)))[:, :-1]
            return jnp.concatenate([t1, t2], axis=-1)

        def l2norm(t):
            return t / jnp.clip(jnp.linalg.norm(t, axis=-1, keepdims=True), 1e-12)

        def rotate_half(x):
            x1, x2 = jnp.split(x, 2, axis=-1)
            return jnp.concatenate([-x2, x1], axis=-1)

        def rotary_xpos(q, k):
            n = q.shape[-2]
            half_idx = jnp.arange(0, DIM_HEAD, 2, dtype=jnp.float32)
            inv_freq = 1.0 / 10000.0 ** (half_idx / DIM_HEAD)
            t = jnp.arange(n, dtype=jnp.float32)
            freqs = t[:, None] * inv_freq[None, :]
            freqs = jnp.concatenate([freqs, freqs], axis=-1)
            base = (half_idx + 0.4 * DIM_HEAD) / (1.4 * DIM_HEAD)
            power = (t - n // 2) / float(WINDOW // 2)
            scale = base[None, :] ** power[:, None]
            scale = jnp.concatenate([scale, scale], axis=-1)
            cos, sin = (jnp.cos(freqs), jnp.sin(freqs))
            q = q * cos * scale + rotate_half(q) * sin * scale
            k = k * cos / scale + rotate_half(k) * sin / scale
            return (q, k)

        def local_attention(q, k, v):
            b, h, n, d = q.shape
            w = n // WINDOW
            bq = q.reshape(b, h, w, WINDOW, d) * QK_SCALE
            bk = k.reshape(b, h, w, WINDOW, d)
            bv = v.reshape(b, h, w, WINDOW, d)

            def look_around(t):
                p = jnp.pad(t, ((0, 0), (0, 0), (1, 0), (0, 0), (0, 0)))
                return jnp.concatenate([p[:, :, :w], p[:, :, 1:]], axis=3)
            bk, bv = (look_around(bk), look_around(bv))
            bt = jnp.arange(n).reshape(w, WINDOW)
            btp = jnp.pad(bt, ((1, 0), (0, 0)), constant_values=-1)
            btk = jnp.concatenate([btp[:w], btp[1:]], axis=1)
            sim = jnp.einsum('bhwid,bhwjd->bhwij', bq, bk)
            i = bt[:, :, None]
            j = btk[:, None, :]
            mask = (i < j) | (i > j + WINDOW) | (j == -1)
            sim = jnp.where(mask, -jnp.finfo(sim.dtype).max, sim)
            attn = jax.nn.softmax(sim, axis=-1)
            out = jnp.einsum('bhwij,bhwjd->bhwid', attn, bv)
            return out.reshape(b, h, n, d)

        def _layer(x, wqkv, qs, ksc, wo, lg, lb, w1, b1, w2, b2):
            b, n, _ = x.shape
            h = shift_token(x)
            qkv = h @ wqkv
            q, k, v = jnp.split(qkv, 3, axis=-1)
            to_heads = lambda t: t.reshape(b, n, HEADS, DIM_HEAD).transpose(0, 2, 1, 3)
            q, k, v = (to_heads(q), to_heads(k), to_heads(v))
            q = l2norm(q) * qs
            k = l2norm(k) * ksc
            q, k = rotary_xpos(q, k)
            o = local_attention(q, k, v)
            o = o.transpose(0, 2, 1, 3).reshape(b, n, INNER)
            x = x + o @ wo
            h = shift_token(x)
            mu = h.mean(-1, keepdims=True)
            var = h.var(-1, keepdims=True)
            h = (h - mu) / jnp.sqrt(var + 1e-05) * lg + lb
            h = h @ w1 + b1
            a, g = jnp.split(h, 2, axis=-1)
            h = a * jax.nn.gelu(g, approximate=False)
            x = x + h @ w2 + b2
            return x
        key = jax.random.key(seed)
        ks = jax.random.split(key, 6)
        return {'x': jax.random.normal(ks[0], (B, N, DIM), jnp.float32), 'wqkv': jax.random.normal(ks[1], (DEPTH, DIM, 3 * INNER), jnp.float32) * 0.02, 'q_scale': jnp.ones((DEPTH, DIM_HEAD), jnp.float32), 'k_scale': jnp.ones((DEPTH, DIM_HEAD), jnp.float32), 'wo': jax.random.normal(ks[2], (DEPTH, INNER, DIM), jnp.float32) * 0.02, 'ln_g': jnp.ones((DEPTH, DIM), jnp.float32), 'ln_b': jnp.zeros((DEPTH, DIM), jnp.float32), 'w1': jax.random.normal(ks[3], (DEPTH, DIM, 2 * HID), jnp.float32) * 0.02, 'b1': jnp.zeros((DEPTH, 2 * HID), jnp.float32), 'w2': jax.random.normal(ks[4], (DEPTH, HID, DIM), jnp.float32) * 0.02, 'b2': jnp.zeros((DEPTH, DIM), jnp.float32)}
    _L0_ffn_in = _L0_ffn_setup()
    _d = {'L0_attn_x': _L0_attn_in['x'], 'L0_attn_gamma': _L0_attn_in['gamma'], 'L0_attn_W_qkv': _L0_attn_in['W_qkv'], 'L0_attn_W_gates': _L0_attn_in['W_gates'], 'L0_attn_b_gates': _L0_attn_in['b_gates'], 'L0_attn_W_out': _L0_attn_in['W_out'], 'L0_ffn_wqkv': _L0_ffn_in['wqkv'], 'L0_ffn_q_scale': _L0_ffn_in['q_scale'], 'L0_ffn_k_scale': _L0_ffn_in['k_scale'], 'L0_ffn_wo': _L0_ffn_in['wo'], 'L0_ffn_ln_g': _L0_ffn_in['ln_g'], 'L0_ffn_ln_b': _L0_ffn_in['ln_b'], 'L0_ffn_w1': _L0_ffn_in['w1'], 'L0_ffn_b1': _L0_ffn_in['b1'], 'L0_ffn_w2': _L0_ffn_in['w2'], 'L0_ffn_b2': _L0_ffn_in['b2']}
    _x0 = _d['L0_attn_x']
    _d['L0_attn_x'] = jax.random.normal(jax.random.fold_in(jax.random.key(seed), 1), (4, 1024, 256), dtype=_x0.dtype)
    del _x0
    return _d

def reference(L0_attn_x, L0_attn_gamma, L0_attn_W_qkv, L0_attn_W_gates, L0_attn_b_gates, L0_attn_W_out, L0_ffn_wqkv, L0_ffn_q_scale, L0_ffn_k_scale, L0_ffn_wo, L0_ffn_ln_g, L0_ffn_ln_b, L0_ffn_w1, L0_ffn_b1, L0_ffn_w2, L0_ffn_b2):

    def _L0_attn_ref(x, gamma, W_qkv, W_gates, b_gates, W_out):
        import jax, jax.numpy as jnp
        import numpy as np
        DIM = 256
        HEADS = 16
        DIM_HEAD = 64
        WINDOW = 64
        NEG = -1000000000.0

        def rms_norm(x, gamma, size):
            nrm = jnp.sqrt(jnp.sum(x * x, axis=-1, keepdims=True))
            return x / jnp.maximum(nrm, 1e-12) * size ** 0.5 * gamma

        def sliding_window_attention(q, k, v, window):
            b, h, S, d = q.shape
            Bk = window
            nb = S // Bk
            qb = q.reshape(b, h, nb, Bk, d)
            kb = k.reshape(b, h, nb, Bk, d)
            vb = v.reshape(b, h, nb, Bk, d)
            k_prev = jnp.pad(kb, ((0, 0), (0, 0), (1, 0), (0, 0), (0, 0)))[:, :, :nb]
            v_prev = jnp.pad(vb, ((0, 0), (0, 0), (1, 0), (0, 0), (0, 0)))[:, :, :nb]
            kctx = jnp.concatenate([k_prev, kb], axis=3)
            vctx = jnp.concatenate([v_prev, vb], axis=3)
            scale = 1.0 / jnp.sqrt(jnp.asarray(d, q.dtype))
            scores = jnp.einsum('bhnqd,bhnkd->bhnqk', qb, kctx) * scale
            qi = jnp.arange(Bk)[:, None]
            kj = jnp.arange(2 * Bk)[None, :]
            diff = Bk + qi - kj
            base = (diff >= 0) & (diff <= window)
            blk = jnp.arange(nb)[:, None, None]
            key_exists = (blk - 1) * Bk + kj[None] >= 0
            mask = base[None] & key_exists
            scores = jnp.where(mask[None, None], scores, NEG)
            attn = jax.nn.softmax(scores, axis=-1)
            out = jnp.einsum('bhnqk,bhnkd->bhnqd', attn, vctx)
            return out.reshape(b, h, S, d)
        b, S, dim = x.shape
        xn = rms_norm(x, gamma, dim)
        qkv = xn @ W_qkv
        qkv = qkv.reshape(b, S, 3, HEADS, DIM_HEAD)
        q, k, v = [jnp.transpose(t, (0, 2, 1, 3)) for t in (qkv[:, :, 0], qkv[:, :, 1], qkv[:, :, 2])]
        out = sliding_window_attention(q, k, v, WINDOW)
        gates = xn @ W_gates + b_gates
        out = out * jax.nn.sigmoid(jnp.transpose(gates, (0, 2, 1)))[..., None]
        out = jnp.transpose(out, (0, 2, 1, 3)).reshape(b, S, HEADS * DIM_HEAD)
        return out @ W_out

    def _L0_ffn_ref(x, wqkv, q_scale, k_scale, wo, ln_g, ln_b, w1, b1, w2, b2):
        import jax, jax.numpy as jnp
        import numpy as np
        DIM = 256
        DEPTH = 2
        HEADS = 8
        DIM_HEAD = 64
        WINDOW = 128
        INNER = HEADS * DIM_HEAD
        HID = int(DIM * 4 * 2 / 3)
        B, N = (2, 2048)
        QK_SCALE = 8.0

        def shift_token(t):
            t1, t2 = jnp.split(t, 2, axis=-1)
            t2 = jnp.pad(t2, ((0, 0), (1, 0), (0, 0)))[:, :-1]
            return jnp.concatenate([t1, t2], axis=-1)

        def l2norm(t):
            return t / jnp.clip(jnp.linalg.norm(t, axis=-1, keepdims=True), 1e-12)

        def rotate_half(x):
            x1, x2 = jnp.split(x, 2, axis=-1)
            return jnp.concatenate([-x2, x1], axis=-1)

        def rotary_xpos(q, k):
            n = q.shape[-2]
            half_idx = jnp.arange(0, DIM_HEAD, 2, dtype=jnp.float32)
            inv_freq = 1.0 / 10000.0 ** (half_idx / DIM_HEAD)
            t = jnp.arange(n, dtype=jnp.float32)
            freqs = t[:, None] * inv_freq[None, :]
            freqs = jnp.concatenate([freqs, freqs], axis=-1)
            base = (half_idx + 0.4 * DIM_HEAD) / (1.4 * DIM_HEAD)
            power = (t - n // 2) / float(WINDOW // 2)
            scale = base[None, :] ** power[:, None]
            scale = jnp.concatenate([scale, scale], axis=-1)
            cos, sin = (jnp.cos(freqs), jnp.sin(freqs))
            q = q * cos * scale + rotate_half(q) * sin * scale
            k = k * cos / scale + rotate_half(k) * sin / scale
            return (q, k)

        def local_attention(q, k, v):
            b, h, n, d = q.shape
            w = n // WINDOW
            bq = q.reshape(b, h, w, WINDOW, d) * QK_SCALE
            bk = k.reshape(b, h, w, WINDOW, d)
            bv = v.reshape(b, h, w, WINDOW, d)

            def look_around(t):
                p = jnp.pad(t, ((0, 0), (0, 0), (1, 0), (0, 0), (0, 0)))
                return jnp.concatenate([p[:, :, :w], p[:, :, 1:]], axis=3)
            bk, bv = (look_around(bk), look_around(bv))
            bt = jnp.arange(n).reshape(w, WINDOW)
            btp = jnp.pad(bt, ((1, 0), (0, 0)), constant_values=-1)
            btk = jnp.concatenate([btp[:w], btp[1:]], axis=1)
            sim = jnp.einsum('bhwid,bhwjd->bhwij', bq, bk)
            i = bt[:, :, None]
            j = btk[:, None, :]
            mask = (i < j) | (i > j + WINDOW) | (j == -1)
            sim = jnp.where(mask, -jnp.finfo(sim.dtype).max, sim)
            attn = jax.nn.softmax(sim, axis=-1)
            out = jnp.einsum('bhwij,bhwjd->bhwid', attn, bv)
            return out.reshape(b, h, n, d)

        def _layer(x, wqkv, qs, ksc, wo, lg, lb, w1, b1, w2, b2):
            b, n, _ = x.shape
            h = shift_token(x)
            qkv = h @ wqkv
            q, k, v = jnp.split(qkv, 3, axis=-1)
            to_heads = lambda t: t.reshape(b, n, HEADS, DIM_HEAD).transpose(0, 2, 1, 3)
            q, k, v = (to_heads(q), to_heads(k), to_heads(v))
            q = l2norm(q) * qs
            k = l2norm(k) * ksc
            q, k = rotary_xpos(q, k)
            o = local_attention(q, k, v)
            o = o.transpose(0, 2, 1, 3).reshape(b, n, INNER)
            x = x + o @ wo
            h = shift_token(x)
            mu = h.mean(-1, keepdims=True)
            var = h.var(-1, keepdims=True)
            h = (h - mu) / jnp.sqrt(var + 1e-05) * lg + lb
            h = h @ w1 + b1
            a, g = jnp.split(h, 2, axis=-1)
            h = a * jax.nn.gelu(g, approximate=False)
            x = x + h @ w2 + b2
            return x
        for l in range(DEPTH):
            x = _layer(x, wqkv[l], q_scale[l], k_scale[l], wo[l], ln_g[l], ln_b[l], w1[l], b1[l], w2[l], b2[l])
        return x
    x = L0_attn_x
    xn = _layernorm(x, axis=-1)
    x = x + _L0_attn_ref(xn, L0_attn_gamma, L0_attn_W_qkv, L0_attn_W_gates, L0_attn_b_gates, L0_attn_W_out) + _L0_ffn_ref(xn, L0_ffn_wqkv, L0_ffn_q_scale, L0_ffn_k_scale, L0_ffn_wo, L0_ffn_ln_g, L0_ffn_ln_b, L0_ffn_w1, L0_ffn_b1, L0_ffn_w2, L0_ffn_b2)
    return x

_drawn_inputs = setup_inputs


def setup_inputs(seed=0):
    import zlib

    import numpy as np

    out = dict(_drawn_inputs(seed))
    spreads = {'L0_attn_gamma': (1.0, 0.6),
     'L0_attn_b_gates': (0.0, 0.8),
     'L0_ffn_q_scale': (1.0, 0.6),
     'L0_ffn_k_scale': (1.0, 0.6),
     'L0_ffn_ln_g': (1.0, 0.6),
     'L0_ffn_ln_b': (0.0, 2.0),
     'L0_ffn_b1': (0.0, 0.8),
     'L0_ffn_b2': (0.0, 0.365)}
    factors = {'L0_attn_W_qkv': 7.576,
     'L0_attn_W_gates': 8.0,
     'L0_attn_W_out': 7.579,
     'L0_ffn_wqkv': 3.387,
     'L0_ffn_wo': 3.315}
    for name, (base, spread) in spreads.items():
        noise = np.random.default_rng([zlib.crc32(name.encode()), seed]).standard_normal(out[name].shape)
        drawn = base * np.exp(spread * noise) if base else spread * noise
        out[name] = jnp.asarray(drawn.astype(out[name].dtype))
    for name, factor in factors.items():
        out[name] = (out[name] * factor).astype(out[name].dtype)
    return out
```

```python
from contextlib import ExitStack

import numpy as np
from concourse import mybir

F32 = mybir.dt.float32
F32R = mybir.dt.float32r
ALU = mybir.AluOpType
ACT = mybir.ActivationFunctionType
AXIS = mybir.AxisListType

P = 128
D = 256
CT = D // P
DH = 64
SEQ = 1024
BATCH = 4
TILES = 4
CHUNK = TILES * P
HALVES = SEQ // CHUNK
CHUNKS = BATCH * HALVES
PAIRS = 4
GROUP = 2 * PAIRS
GC = GROUP * DH
UNITS = 2 * PAIRS
HI, LO = 0, 1
PASSES = ((HI, HI), (HI, LO), (LO, HI))
MASKED = -1e30
VALUE, ZERO, VALUE_2 = range(3)

A_HEADS, A_WINDOW = 16, 64
A_GROUPS = A_HEADS // GROUP
A_INNER = A_HEADS * DH


def numbered(steps, sizes):
    first, n = {}, 0
    for step in steps:
        if step[0] in sizes:
            first[step] = n
            n += sizes[step[0]]
    return first, n


class Count:

    def __init__(self, sem, before, steps, sizes, unit=1, credit=0):
        self.sem, self.unit, self.credit = sem, unit, credit
        self.first0, self.before = numbered(before, sizes)
        self.first, self.each = numbered(steps, sizes)

    def number(self, it, step, i=0):
        return (self.first0 if it is None else self.first)[step] + i

    def past(self, it, step, i=0):
        return self.upto(it, self.number(it, step, i))

    def upto(self, it, n):
        if it is None:
            return self.credit + self.unit * (n + 1)
        return it * (self.unit * self.each) + (self.credit + self.unit * (self.before + n + 1))


def key_tiles(half):
    for kt in range(-1 if half else 0, TILES):
        yield kt, max(2 * kt + 1, 0) * P, min(2 * kt + 3, 2 * TILES) * P, max(kt, 0) * P, min(kt + 2, TILES) * P


def tokens_of(state, sequence, half, ahead=0):
    return state[sequence, ahead + half * CHUNK:ahead + (half + 1) * CHUNK, :].rearrange("(t p) d -> p t d", p=P)


def attention_phase(nc, x, gamma, w_qkv, w_gates, b_gates, w_out, masks, identity, normed, hidden, attended):
    with ExitStack() as ctx:
        def sb(name, shape, dt=F32):
            return ctx.enter_context(nc.sbuf_tensor("a_" + name, shape, dt))

        BLOCKS = HALVES * A_GROUPS
        NU = BLOCKS * UNITS
        NP = BLOCKS * PAIRS
        K0 = P - A_WINDOW
        KEYS = A_WINDOW + P

        wqkv = sb("wqkv", [P, 2, CT, 3 * A_INNER], F32R)
        wout = sb("wout", [P, 2, A_INNER // P, D], F32R)
        wgate = sb("wgate", [P, 2, CT, A_HEADS], F32R)
        ident = sb("ident", [P, P])
        mask = sb("mask", [P, 2, KEYS])
        gamma_row = sb("gamma_row", [P, D])
        bgate_row = sb("bgate_row", [P, A_HEADS])
        zero_rows = sb("zero_rows", [BATCH, D])
        minus_half = sb("minus_half", [P, TILES])
        x_tok = sb("x_tok", [P, TILES, D])
        xT = sb("xT", [P, 2, CT, CHUNK], F32R)
        q_o = sb("q_o", [P, A_GROUPS, 2, PAIRS, CHUNK], F32R)
        kT = sb("kT", [P, 2, PAIRS, A_WINDOW + CHUNK], F32R)
        k_kept = sb("k_kept", [P, A_GROUPS, 2, PAIRS, A_WINDOW], F32R)
        v = sb("v", [P, TILES, 2, PAIRS, 3, DH], F32R)
        v_kept = sb("v_kept", [P, A_GROUPS, 2, PAIRS, 3, DH], F32R)
        probT = sb("probT", [P, 2, 2, 2 * TILES * P], F32R)
        prob = sb("prob", [P, 2, 2, 2, 2 * P])
        y_tok = sb("y_tok", [P, TILES, D])
        square = sb("square", [P, D], mybir.dt.bfloat16)
        bn = sb("bn", [P, TILES, 6])
        mean_var = sb("mean_var", [P, TILES, 2])
        rstd = sb("rstd", [P, TILES])
        sumsq = sb("sumsq", [P, TILES])
        rms = sb("rms", [P, TILES])
        gate_in = sb("gate_in", [P, TILES, A_HEADS])
        gate = sb("gate", [P, HALVES, TILES, A_HEADS])
        row_max = sb("row_max", [P, 2, 2, 2])
        neg_max = sb("neg_max", [P, 2, 2, 2])
        row_sum = sb("row_sum", [P, 2, 2, 2])
        row_inv = sb("row_inv", [P, 2, 2, 2])
        weight = sb("weight", [P, 2, 2, 2])
        stage = prob[:].rearrange("p a b c d -> p (a b c d)").rearrange("p (s n) -> p s n", s=2)
        scores = [[ctx.enter_context(nc.psum_tensor(f"a_scores{i}{h}", [P, 2, 2 * P], F32)) for h in (0, 1)] for i in (0, 1)]
        bank = [ctx.enter_context(nc.psum_tensor(f"a_bank{i}", [P, 512], F32)) for i in range(3)]
        o_bank = ctx.enter_context(nc.psum_tensor("a_o_bank", [P, CHUNK], F32))

        prepare = {2: "load_x", 4: "norm_stats", 5: "norm_apply", 6: "rms_sum", 7: "rms_scale", 9: "rms_apply",
                   12: "transpose_x", 13: "gates"}
        steps = []
        for s in range(NU + 4):
            k, r = divmod(s, UNITS)
            if r == 0 and k >= 1:
                steps.append(("project_qk", k))
            if r == 0 and A_GROUPS <= k < BLOCKS:
                steps.append(("keys_back", k))
            if s < NU:
                steps.append(("scores", s))
            if s % (2 * UNITS) == 4 and s < NU:
                steps.append(("load_y", s // (2 * UNITS)))
            if s >= 4 and s % 2 == 0:
                steps.append(("values", (s - 4) // 2))
            if 2 <= s < NU + 2:
                steps.append(("transpose", s - 2))
            if s < NU:
                steps.append(("softmax", s))
            if r == 0 and k < A_GROUPS:
                steps.append(("keep_keys", k))
            if s < NU:
                steps.append(("weigh", s))
            if s == 1 or (r == 2 and 1 <= k < BLOCKS):
                steps.append(("project_v", k))
            if r == 3 and k >= 1:
                steps.append(("project_out", k - 1))
            for h in range(HALVES):
                if s - 2 * UNITS * h in prepare:
                    steps.append((prepare[s - 2 * UNITS * h], h))
        before = [(kind, HALVES - 1) for kind in prepare.values()] + [("project_qk", BLOCKS)]

        def count(name, sizes, unit=1, credit=0):
            return Count(nc.alloc_semaphore("a_" + name), before, steps, sizes, unit, credit)

        fills = {"project_qk": 2 * PAIRS, "project_v": TILES, "project_out": TILES, "transpose": 2, "transpose_x": CT, "gates": 1}
        highs = {kind: n for kind, n in fills.items() if kind not in ("project_out", "gates")}
        filled = count("filled", fills)
        hi_taken = count("hi_taken", highs)
        emptied = count("emptied", fills)
        scored = count("scored", {"scores": 1})
        maxed = count("maxed", {"scores": 2})
        negated = count("negated", {"scores": 2})
        exped = count("exped", {"scores": 2}, credit=1)
        inverted = count("inverted", {"weigh": 2})
        weighed = count("weighed", {"weigh": 2})
        normalized = count("normalized", {"weigh": 2})
        o_filled = count("o_filled", {"values": 1})
        o_hi_taken = count("o_hi_taken", {"values": 1})
        o_emptied = count("o_emptied", {"values": 1}, credit=1)
        x_loaded = count("x_loaded", {"load_x": 1}, unit=16)
        bn_done = count("bn_done", {"norm_stats": 1})
        aggregated = count("aggregated", {"norm_stats": 1})
        var_ready = count("var_ready", {"norm_stats": 1})
        rstd_ready = count("rstd_ready", {"norm_stats": 1})
        x_normed = count("x_normed", {"norm_apply": 1})
        normed_stored = count("normed_stored", {"norm_apply": 1}, unit=16)
        squared = count("squared", {"rms_sum": TILES})
        ms_ready = count("ms_ready", {"rms_scale": 1})
        rms_ready = count("rms_ready", {"rms_scale": 1})
        x_ready = count("x_ready", {"rms_apply": 1})
        gate_biased = count("gate_biased", {"gates": 1})
        gate_exped = count("gate_exped", {"gates": 1})
        gate_plus_1 = count("gate_plus_1", {"gates": 1})
        gated = count("gated", {"gates": 1})
        keys_kept = count("keys_kept", {"keep_keys": 1}, unit=16)
        keys_back = count("keys_back", {"keys_back": 1}, unit=16)
        y_loaded = count("y_loaded", {"load_y": 1}, unit=16)
        y_stored = count("y_stored", {"load_y": 1}, unit=16, credit=1)
        consts_loaded = nc.alloc_semaphore("a_consts_loaded")
        staged = [nc.alloc_semaphore(f"a_staged{i}") for i in (0, 1)]
        stage_hi_taken = nc.alloc_semaphore("a_stage_hi_taken")
        stage_emptied = nc.alloc_semaphore("a_stage_emptied")
        dve_carried, sp_carried = nc.alloc_semaphore("a_dve_carried"), nc.alloc_semaphore("a_sp_carried")
        zero_rows_ready = nc.alloc_semaphore("a_zero_rows_ready")
        zero_rows_stored = nc.alloc_semaphore("a_zero_rows_stored")
        zeroed = nc.alloc_semaphore("a_zeroed")
        CONSTS = 4

        pieces = []
        for c in range(CT):
            for n in range(3):
                cols = slice(n * A_INNER, (n + 1) * A_INNER)
                pieces.append((w_qkv[c * P:(c + 1) * P, cols], wqkv[:, HI, c, cols], wqkv[:, LO, c, cols]))
        wo_rows = w_out.rearrange("(c p) n -> p c n", p=P)
        for c in range(0, A_INNER // P, 4):
            pieces.append((wo_rows[:, c:c + 4, :], wout[:, HI, c:c + 4, :], wout[:, LO, c:c + 4, :]))
        pieces.append((w_gates.rearrange("(c p) n -> p c n", p=P), wgate[:, HI], wgate[:, LO]))

        def stage_of(i):
            shape = pieces[i][1].shape
            if len(shape) == 2:
                return stage[:, i % 2, 0:shape[1]]
            return stage[:, i % 2, 0:shape[1] * shape[2]].rearrange("p (c n) -> p c n", n=shape[2])

        def prepared(it, h):
            return 0 if it is None else (it + (h + 1) // HALVES) % BATCH, (h + 1) % HALVES

        def half_group(k):
            return (k // A_GROUPS) % HALVES, k % A_GROUPS

        def unit_place(u):
            return u // UNITS, u % UNITS // 2, 2 * (u % 2)

        def values_of(half, group, tile):
            return v_kept[:, group] if tile < 0 or (half == 0 and tile == TILES - 1) else v[:, tile]

        def value_operand(half, group, tile, part, pair, head):
            return values_of(half, group, tile)[:, part, pair, head:head + 2, :].rearrange("p b d -> p (b d)")

        def like(source, place):
            if len(place.shape) == 2:
                return source[:]
            return source[:].rearrange("p (a b d) -> p a b d", a=place.shape[1], b=place.shape[2])

        block = ctx.enter_context(nc.Block())

        @block.sync
        def _(sp):
            sp.dma_start(ident[:], identity).then_inc(consts_loaded, 16)
            sp.dma_start(mask[:], masks.rearrange("s p k -> p s k")[:, :, K0:2 * P]).then_inc(consts_loaded, 16)
            sp.dma_start(gamma_row[:], gamma.unsqueeze(0).broadcast_to([P, D])).then_inc(consts_loaded, 16)
            sp.dma_start(bgate_row[:], b_gates.unsqueeze(0).broadcast_to([P, A_HEADS])).then_inc(consts_loaded, 16)
            sp.sem_inc(y_stored.sem, 1)

            def load_x(it, h):
                if it is not None:
                    sp.wait_ge(filled.sem, filled.past(it, ("transpose_x", h - 1), CT - 1) if h else filled.upto(it, -1))
                sequence, half = prepared(it, h)
                sp.dma_start(x_tok[:], tokens_of(x, sequence, half)).then_inc(x_loaded.sem, 16)

            def store_normed(it, h):
                sp.wait_ge(x_normed.sem, x_normed.past(it, ("norm_apply", h)))
                sequence, half = prepared(it, h)
                sp.dma_start(tokens_of(normed, sequence, half, ahead=1), x_tok[:]).then_inc(normed_stored.sem, 16)

            load_x(None, HALVES - 1)
            for i, (src, _, _) in enumerate(pieces):
                if i >= 2:
                    sp.wait_ge(stage_emptied, i - 1)
                sp.dma_start(stage_of(i), src).then_inc(staged[i % 2], 16)
            sp.wait_ge(zero_rows_ready, 1)
            for state in (normed, hidden):
                sp.dma_start(state[:, 0, :], zero_rows[:]).then_inc(zero_rows_stored, 16)
            store_normed(None, HALVES - 1)
            with sp.Fori(0, BATCH) as it:
                for step in steps:
                    kind, a = step
                    if kind == "load_x":
                        load_x(it, a)
                    elif kind == "norm_apply":
                        store_normed(it, a)
                    elif kind == "load_y":
                        sp.wait_ge(y_stored.sem, y_stored.upto(it, a - 1))
                        sp.sem_inc(sp_carried, 1)
                        sp.dma_start(y_tok[:], tokens_of(x, it, a)).then_inc(y_loaded.sem, 16)
                    elif kind == "keep_keys":
                        sp.wait_ge(emptied.sem, emptied.past(it, ("project_qk", a), 2 * PAIRS - 1) if a else emptied.upto(it, -1))
                        sp.dma_start(k_kept[:, a].bitcast(F32), kT[:, :, :, CHUNK:CHUNK + A_WINDOW].bitcast(F32)).then_inc(keys_kept.sem, 16)
                    elif kind == "keys_back":
                        sp.wait_ge(scored.sem, scored.past(it, ("scores", UNITS * a - 1)))
                        sp.dma_start(kT[:, :, :, 0:A_WINDOW].bitcast(F32), k_kept[:, a % A_GROUPS].bitcast(F32)).then_inc(keys_back.sem, 16)
                    elif kind == "project_out" and a % A_GROUPS == A_GROUPS - 1:
                        sp.wait_ge(emptied.sem, emptied.past(it, step, TILES - 1))
                        sp.dma_start(tokens_of(attended, it, a // A_GROUPS), y_tok[:]).then_inc(y_stored.sem, 16)
            sp.wait_ge(y_stored.sem, y_stored.upto(BATCH, -1))
            sp.wait_ge(normed_stored.sem, normed_stored.upto(BATCH, -1))
            sp.wait_ge(zero_rows_stored, 16 * 2)

        @block.gpsimd
        def _(pool):
            pool.memset(zero_rows[:], 0.0).then_inc(zero_rows_ready, 1)
            pool.memset(minus_half[:], -0.5)
            pool.memset(kT[:, :, :, 0:A_WINDOW].bitcast(F32), 0.0)
            for t in range(TILES):
                for part in (HI, LO):
                    pool.memset(v[:, t, part, :, ZERO, :].bitcast(F32), 0.0)
            for group in range(A_GROUPS):
                for part in (HI, LO):
                    pool.memset(v_kept[:, group, part, :, ZERO, :].bitcast(F32), 0.0)
            pool.wait_ge(stage_emptied, len(pieces))
            pool.memset(prob[:, :, :, :, 0:K0], 0.0).then_inc(zeroed, 1)

            def power(it, h):
                pool.wait_ge(var_ready.sem, var_ready.past(it, ("norm_stats", h)))
                nc.gpsimd.tensor_tensor(rstd[:], rstd[:], minus_half[:], ALU.pow).then_inc(rstd_ready.sem, 1)

            def rms_power(it, h):
                pool.wait_ge(ms_ready.sem, ms_ready.past(it, ("rms_scale", h)))
                nc.gpsimd.tensor_tensor(rms[:], rms[:], minus_half[:], ALU.pow).then_inc(rms_ready.sem, 1)

            pool.wait_ge(zeroed, 1)
            power(None, HALVES - 1)
            rms_power(None, HALVES - 1)
            with pool.Fori(0, BATCH) as it:
                for kind, a in steps:
                    if kind == "norm_stats":
                        power(it, a)
                    elif kind == "rms_scale":
                        rms_power(it, a)
                    elif kind == "weigh":
                        for head in (0, 1):
                            pool.wait_ge(weighed.sem, weighed.past(it, (kind, a), head))
                            part = prob[:, a % 2, head, :, K0:2 * P]
                            nc.gpsimd.tensor_tensor(part, part, weight[:, a % 2, head].unsqueeze(2).broadcast_to([P, 2, KEYS]),
                                                    ALU.mult).then_inc(normalized.sem, 1)

        @block.tensor
        def _(pe):
            def take_bank(it, n):
                if n >= 3 or it is not None:
                    pe.wait_ge(emptied.sem, emptied.upto(it, n - 3 if n >= 3 else -1))
                return bank[n % 3]

            def products(out, lhs, rhs, tiles):
                order = [(c, a, b) for c in range(tiles) for a, b in PASSES]
                for i, (c, a, b) in enumerate(order):
                    last = nc.tensor.matmul(out, lhs(c, a), rhs(c, b), start=(i == 0), stop=(i == len(order) - 1))
                return last

            def transpose_x(it, h):
                pe.wait_ge(x_ready.sem, x_ready.past(it, ("rms_apply", h)))
                for c in range(CT):
                    out = take_bank(it, filled.number(it, ("transpose_x", h), c))
                    for t in range(TILES):
                        last = nc.tensor.transpose(out[:, t * P:(t + 1) * P], x_tok[:, t, c * P:(c + 1) * P], ident[:])
                    last.then_inc(filled.sem, 1)

            def gates(it, h):
                pe.wait_ge(emptied.sem, emptied.past(it, ("transpose_x", h), CT - 1))
                out = take_bank(it, filled.number(it, ("gates", h)))
                for t in range(TILES):
                    last = products(out[:, t * A_HEADS:(t + 1) * A_HEADS], lambda c, part: xT[:, part, c, t * P:(t + 1) * P],
                                    lambda c, part: wgate[:, part, c, :], CT)
                last.then_inc(filled.sem, 1)

            def project_qk(it, k):
                _, group = half_group(k)
                for i in range(2 * PAIRS):
                    pair, which = divmod(i, 2)
                    out = take_bank(it, filled.number(it, ("project_qk", k), i))
                    col = which * A_INNER + (group * PAIRS + pair) * P
                    products(out[:], lambda c, part: wqkv[:, part, c, col:col + P], lambda c, part: xT[:, part, c, :],
                             CT).then_inc(filled.sem, 1)

            pe.wait_ge(consts_loaded, 16 * CONSTS)
            transpose_x(None, HALVES - 1)
            pe.wait_ge(stage_emptied, len(pieces))
            gates(None, HALVES - 1)
            project_qk(None, BLOCKS)
            pe.wait_ge(zeroed, 1)
            with pe.Fori(0, BATCH) as it:
                for kind, a in steps:
                    if kind == "project_qk":
                        project_qk(it, a)
                    elif kind == "scores":
                        k, pair, tile = unit_place(a)
                        half, group = half_group(k)
                        if a % UNITS == 0:
                            pe.wait_ge(emptied.sem, emptied.past(it, ("project_qk", k), 2 * PAIRS - 1) if k else emptied.upto(it, -1))
                            if half:
                                pe.wait_ge(keys_back.sem, keys_back.past(it, ("keys_back", k)))
                        pe.wait_ge(exped.sem, exped.past(it, ("scores", a - 2), 1) if a >= 2 else exped.upto(it, -1))
                        for t in (0, 1):
                            col = (tile + t) * P
                            for i, (qp, kp) in enumerate(PASSES):
                                for head in (0, 1):
                                    rows = slice(DH * head, DH * (head + 1))
                                    mm = nc.tensor.matmul(scores[a % 2][head][:, t, K0:2 * P], q_o[rows, group, qp, pair, col:col + P],
                                                          kT[rows, kp, pair, col:col + KEYS], start=(i == 0), stop=(i == 2))
                        mm.then_inc(scored.sem, 1)
                    elif kind == "transpose":
                        for head in (0, 1):
                            out = take_bank(it, filled.number(it, (kind, a), head))
                            pe.wait_ge(normalized.sem, normalized.past(it, ("weigh", a), head))
                            for j in range(4):
                                last = nc.tensor.transpose(out[:, j * P:(j + 1) * P], prob[:, a % 2, head, j // 2, (j % 2) * P:(j % 2 + 1) * P],
                                                           ident[:])
                            last.then_inc(filled.sem, 1)
                    elif kind == "values":
                        k, pair = divmod(a, PAIRS)
                        half, group = half_group(k)
                        pe.wait_ge(emptied.sem, emptied.past(it, ("transpose", 2 * a + 1), 1))
                        pe.wait_ge(o_emptied.sem, o_emptied.upto(it, a - 1))
                        order = [(kt, head, vp, pp) for kt in key_tiles(half) for head in (0, 1) for vp, pp in PASSES]
                        for i, ((tile, p0, p1, o0, o1), head, vp, pp) in enumerate(order):
                            mm = nc.tensor.matmul(o_bank[:, o0:o1], value_operand(half, group, tile, vp, pair, head),
                                                  probT[:, pp, head, p0:p1], start=(i == 0), stop=(i == len(order) - 1),
                                                  skip_group_check=True)
                        mm.then_inc(o_filled.sem, 1)
                    elif kind == "project_v":
                        _, group = half_group(a)
                        for t in range(TILES):
                            out = take_bank(it, filled.number(it, (kind, a), t))
                            col = 2 * A_INNER + group * GC
                            products(out[:], lambda c, part: xT[:, part, c, t * P:(t + 1) * P], lambda c, part: wqkv[:, part, c, col:col + GC],
                                     CT).then_inc(filled.sem, 1)
                    elif kind == "project_out":
                        _, group = half_group(a)
                        pe.wait_ge(o_emptied.sem, o_emptied.past(it, ("values", PAIRS * (a + 1) - 1)))
                        for t in range(TILES):
                            out = take_bank(it, filled.number(it, (kind, a), t))
                            products(out[:, 0:D], lambda c, part: q_o[:, group, part, c, t * P:(t + 1) * P],
                                     lambda c, part: wout[:, part, group * PAIRS + c, :], PAIRS).then_inc(filled.sem, 1)
                    elif kind == "transpose_x":
                        transpose_x(it, a)
                    elif kind == "gates":
                        gates(it, a)

        def high_targets(it, kind, a):
            if kind == "project_qk":
                _, group = half_group(a)
                return [(lambda part, pair=i // 2, which=i % 2: kT[:, part, pair, A_WINDOW:A_WINDOW + CHUNK] if which
                         else q_o[:, group, part, pair, :]) for i in range(2 * PAIRS)]
            if kind == "project_v":
                half, group = half_group(a)
                return [(lambda part, t=t: values_of(half, group, t)[:, part, :, VALUE:VALUE_2 + 1:2, :]) for t in range(TILES)]
            if kind == "transpose":
                return [(lambda part, head=head: probT[:, part, head, a % 2 * 4 * P:(a % 2 + 1) * 4 * P]) for head in (0, 1)]
            assert kind == "transpose_x"
            return [(lambda part, c=c: xT[:, part, c, :]) for c in range(CT)]

        @block.scalar
        def _(act):
            act.sem_inc(exped.sem, 1)
            for i, (_, hi, _) in enumerate(pieces):
                act.wait_ge(staged[i % 2], 16 * (i // 2 + 1))
                nc.scalar.activation(hi, stage_of(i), ACT.Copy).then_inc(stage_hi_taken, 1)

            def take_high(it, kind, a):
                for i, place in enumerate(high_targets(it, kind, a)):
                    n = filled.number(it, (kind, a), i)
                    act.wait_ge(filled.sem, filled.upto(it, n))
                    nc.scalar.activation(place(HI), like(bank[n % 3], place(HI)), ACT.Copy).then_inc(hi_taken.sem, 1)

            def rms_sum(it, h):
                act.wait_ge(x_normed.sem, x_normed.past(it, ("norm_apply", h)))
                for t in range(TILES):
                    if it is not None or t:
                        act.wait_ge(squared.sem, squared.upto(it, squared.number(it, ("rms_sum", h), t) - 1))
                    nc.scalar.activation(square[:], x_tok[:, t, :], ACT.Square, accum_out=sumsq[:, t:t + 1]).then_inc(squared.sem, 1)

            def gates(it, h):
                act.wait_ge(gate_biased.sem, gate_biased.past(it, ("gates", h)))
                nc.scalar.activation(gate_in[:], gate_in[:], ACT.Exp, scale=-1.0).then_inc(gate_exped.sem, 1)

            rms_sum(None, HALVES - 1)
            take_high(None, "transpose_x", HALVES - 1)
            gates(None, HALVES - 1)
            take_high(None, "project_qk", BLOCKS)
            with act.Fori(0, BATCH) as it:
                for kind, a in steps:
                    if kind == "project_qk" and 1 <= a <= A_GROUPS:
                        act.wait_ge(keys_kept.sem, keys_kept.past(it, ("keep_keys", a - 1)))
                    if kind in highs:
                        take_high(it, kind, a)
                    elif kind == "softmax":
                        for head in (0, 1):
                            act.wait_ge(negated.sem, negated.past(it, ("scores", a), head))
                            for t in (0, 1):
                                e = nc.scalar.activation(prob[:, a % 2, head, t, K0:2 * P], scores[a % 2][head][:, t, K0:2 * P], ACT.Exp,
                                                         bias=neg_max[:, a % 2, head, t:t + 1], scale=DH ** -0.5,
                                                         accum_out=row_sum[:, a % 2, head, t:t + 1])
                            e.then_inc(exped.sem, 1)
                    elif kind == "values":
                        _, group = half_group(a // PAIRS)
                        act.wait_ge(o_filled.sem, o_filled.past(it, (kind, a)))
                        nc.scalar.activation(q_o[:, group, HI, a % PAIRS, :], o_bank[:], ACT.Copy).then_inc(o_hi_taken.sem, 1)
                    elif kind == "rms_sum":
                        rms_sum(it, a)
                    elif kind == "gates":
                        gates(it, a)

        @block.vector
        def _(dve):
            dve.sem_inc(o_emptied.sem, 1)
            for i, (_, hi, lo) in enumerate(pieces):
                dve.wait_ge(stage_hi_taken, i + 1)
                nc.vector.tensor_tensor(lo, stage_of(i), hi.bitcast(F32), ALU.subtract).then_inc(stage_emptied, 1)

            def take_low(it, kind, a):
                for i, place in enumerate(high_targets(it, kind, a)):
                    n = filled.number(it, (kind, a), i)
                    dve.wait_ge(hi_taken.sem, hi_taken.past(it, (kind, a), i))
                    nc.vector.tensor_tensor(place(LO), like(bank[n % 3], place(LO)), place(HI).bitcast(F32), ALU.subtract).then_inc(emptied.sem, 1)

            def norm_stats(it, h):
                dve.wait_ge(x_loaded.sem, x_loaded.past(it, ("load_x", h)))
                for t in range(TILES):
                    last = nc.vector.bn_stats(bn[:, t, :], x_tok[:, t, :])
                last.then_inc(bn_done.sem, 1)
                dve.wait_ge(bn_done.sem, bn_done.past(it, ("norm_stats", h)))
                dve.sem_inc(dve_carried, 1)
                for t in range(TILES):
                    last = nc.vector.bn_aggr(mean_var[:, t, :], bn[:, t, :])
                last.then_inc(aggregated.sem, 1)
                dve.wait_ge(aggregated.sem, aggregated.past(it, ("norm_stats", h)))
                nc.vector.tensor_scalar(rstd[:], mean_var[:, :, 1], 1e-5, None, ALU.add).then_inc(var_ready.sem, 1)

            def norm_apply(it, h):
                dve.wait_ge(rstd_ready.sem, rstd_ready.past(it, ("norm_stats", h)))
                for t in range(TILES):
                    last = nc.vector.tensor_scalar(x_tok[:, t, :], x_tok[:, t, :], mean_var[:, t, 0:1], rstd[:, t:t + 1], ALU.subtract, ALU.mult)
                last.then_inc(x_normed.sem, 1)

            def rms_scale(it, h):
                dve.wait_ge(squared.sem, squared.past(it, ("rms_sum", h), TILES - 1))
                nc.vector.tensor_scalar(rms[:], sumsq[:], 1e-24, 1.0 / D, ALU.max, ALU.mult).then_inc(ms_ready.sem, 1)

            def rms_apply(it, h):
                dve.wait_ge(rms_ready.sem, rms_ready.past(it, ("rms_scale", h)))
                dve.wait_ge(normed_stored.sem, normed_stored.past(it, ("norm_apply", h)))
                for t in range(TILES):
                    last = nc.vector.scalar_tensor_tensor(out=x_tok[:, t, :], in0=x_tok[:, t, :], scalar=rms[:, t:t + 1], in1=gamma_row[:],
                                                          op0=ALU.mult, op1=ALU.mult)
                last.then_inc(x_ready.sem, 1)

            def gates(it, h):
                n = filled.number(it, ("gates", h))
                dve.wait_ge(filled.sem, filled.upto(it, n))
                logits = bank[n % 3][:, 0:TILES * A_HEADS].rearrange("p (t h) -> p t h", t=TILES)
                g = nc.vector.tensor_tensor(gate_in[:], logits, bgate_row[:].unsqueeze(1).broadcast_to([P, TILES, A_HEADS]), ALU.add)
                g.then_inc(gate_biased.sem, 1)
                dve.wait_ge(gate_exped.sem, gate_exped.past(it, ("gates", h)))
                nc.vector.tensor_scalar(gate_in[:], gate_in[:], 1.0, None, ALU.add).then_inc(gate_plus_1.sem, 1)
                dve.wait_ge(gate_plus_1.sem, gate_plus_1.past(it, ("gates", h)))
                nc.vector.reciprocal(gate[:, (h + 1) % HALVES], gate_in[:]).then_inc(gated.sem, 1)
                dve.sem_inc(emptied.sem, 1)

            norm_stats(None, HALVES - 1)
            norm_apply(None, HALVES - 1)
            rms_scale(None, HALVES - 1)
            dve.wait_ge(consts_loaded, 16 * CONSTS)
            rms_apply(None, HALVES - 1)
            take_low(None, "transpose_x", HALVES - 1)
            gates(None, HALVES - 1)
            take_low(None, "project_qk", BLOCKS)
            with dve.Fori(0, BATCH) as it:
                for kind, a in steps:
                    if kind == "scores":
                        k, _, tile = unit_place(a)
                        half, _ = half_group(k)
                        dve.wait_ge(scored.sem, scored.past(it, (kind, a)))
                        dve.sem_inc(dve_carried, 1)
                        for head in (0, 1):
                            for t in (0, 1):
                                s = scores[a % 2][head][:, t, K0:2 * P]
                                m = nc.vector.tensor_tensor_reduce(out=s, in0=s, in1=mask[:, min(half * TILES + tile + t, 1)], scale=1.0, scalar=-3e38,
                                                                   op0=ALU.add, op1=ALU.max, accum_out=row_max[:, a % 2, head, t:t + 1])
                            m.then_inc(maxed.sem, 1)
                            dve.wait_ge(maxed.sem, maxed.past(it, (kind, a), head))
                            nc.vector.tensor_scalar(neg_max[:, a % 2, head], row_max[:, a % 2, head], -DH ** -0.5, None,
                                                    ALU.mult).then_inc(negated.sem, 1)
                    elif kind in highs:
                        take_low(it, kind, a)
                    elif kind == "weigh":
                        k, pair, tile = unit_place(a)
                        half, group = half_group(k)
                        if a % (2 * UNITS) == 0:
                            dve.wait_ge(gated.sem, gated.upto(it, half - 1))
                        for head in (0, 1):
                            dve.wait_ge(exped.sem, exped.past(it, ("scores", a), head))
                            nc.vector.reciprocal(row_inv[:, a % 2, head], row_sum[:, a % 2, head]).then_inc(inverted.sem, 1)
                            dve.wait_ge(inverted.sem, inverted.past(it, (kind, a), head))
                            nc.vector.tensor_tensor(weight[:, a % 2, head], row_inv[:, a % 2, head],
                                                    gate[:, half, tile:tile + 2, group * GROUP + 2 * pair + head], ALU.mult).then_inc(weighed.sem, 1)
                    elif kind == "values":
                        _, group = half_group(a // PAIRS)
                        dve.wait_ge(o_hi_taken.sem, o_hi_taken.past(it, (kind, a)))
                        nc.vector.tensor_tensor(q_o[:, group, LO, a % PAIRS, :], o_bank[:], q_o[:, group, HI, a % PAIRS, :].bitcast(F32),
                                                ALU.subtract).then_inc(o_emptied.sem, 1)
                    elif kind == "project_out":
                        half, group = half_group(a)
                        if group == 0:
                            dve.wait_ge(y_loaded.sem, y_loaded.past(it, ("load_y", half)))
                        for t in range(TILES):
                            n = filled.number(it, (kind, a), t)
                            dve.wait_ge(filled.sem, filled.upto(it, n))
                            nc.vector.tensor_tensor(y_tok[:, t, :], bank[n % 3][:, 0:D], y_tok[:, t, :], ALU.add).then_inc(emptied.sem, 1)
                    elif kind == "norm_stats":
                        norm_stats(it, a)
                    elif kind == "norm_apply":
                        norm_apply(it, a)
                    elif kind == "rms_scale":
                        rms_scale(it, a)
                    elif kind == "rms_apply":
                        rms_apply(it, a)
                    elif kind == "gates":
                        gates(it, a)


F_HEADS, F_WINDOW, F_DEPTH = 8, 128, 2
F_INNER = F_HEADS * DH
HID = D * 4 * 2 // 3
FH = 6
HT = -(-HID // FH)
HL = HID - (FH - 1) * HT
QUERY, KEY = 0, 1
COS, SIN = 0, 1


def ffn_phase(nc, layer, state_in, state_out, ahead_out, attended, wqkv_in, q_scale, k_scale, wo_in, ln_g, ln_b, w1_in, b1, w2_in, b2,
              masks, identity, tables_in):
    with ExitStack() as ctx:
        def sb(name, shape, dt=F32):
            return ctx.enter_context(nc.sbuf_tensor(f"f{layer}_{name}", shape, dt))

        NU = HALVES * UNITS

        wqkv = sb("wqkv", [P, 2, CT, 3 * F_INNER], F32R)
        wo = sb("wo", [P, 2, PAIRS, D], F32R)
        w1 = sb("w1", [P, 2, CT, 2 * HID], F32R)
        w2 = sb("w2", [P, 2, FH, D], F32R)
        b1_cols = sb("b1_cols", [P, 2, FH])
        ln_g_row = sb("ln_g_row", [P, D])
        ln_b_row = sb("ln_b_row", [P, D])
        b2_row = sb("b2_row", [P, D])
        scale_rows = sb("scale_rows", [P, 2, 2, DH])
        ident = sb("ident", [P, P])
        mask = sb("mask", [P, 2, 2 * P])
        edge = sb("edge", [1, HALVES, P])
        minus_half = sb("minus_half", [P, 2 * F_HEADS])
        x_tok = sb("x_tok", [P, TILES, D])
        x1 = sb("x1", [P, TILES, D])
        actT = sb("actT", [P, 2, CT, CHUNK], F32R)
        q_o = sb("q_o", [P, 2, PAIRS, CHUNK], F32R)
        kT = sb("kT", [P, 2, PAIRS, P + CHUNK], F32R)
        v = sb("v", [P, TILES, 2, PAIRS, 3, DH], F32R)
        v_kept = sb("v_kept", [P, 2, PAIRS, 3, DH], F32R)
        probT = sb("probT", [P, 2, 2, 2 * TILES * P], F32R)
        prob = sb("prob", [P, 2, 2, 2, 2 * P])
        tables = sb("tables", [P, 2, 2, TILES, DH])
        qk_tok = sb("qk_tok", [P, 2, 2, F_INNER])
        square = sb("square", [P, 2, F_INNER])
        cos_part = sb("cos_part", [P, 2, F_INNER])
        sin_part = sb("sin_part", [P, 2, F_INNER])
        gu = sb("gu", [P, 2, CHUNK])
        norm = sb("norm", [P, 2, 2, F_HEADS])
        bn = sb("bn", [P, TILES, 2, 6])
        mean_var = sb("mean_var", [P, TILES, 2])
        rstd = sb("rstd", [P, TILES])
        row_max = sb("row_max", [P, 2, 2, 2])
        neg_max = sb("neg_max", [P, 2, 2, 2])
        row_sum = sb("row_sum", [P, 2, 2, 2])
        weight = sb("weight", [P, 2, 2, 2])
        stage = prob[:].rearrange("p a b c d -> p (a b c d)").rearrange("p (s n) -> p s n", s=2)
        u = probT[:].rearrange("p a b c -> p (a b c)").rearrange("p (s a n) -> p s a n", s=4, a=2)
        scores = [[ctx.enter_context(nc.psum_tensor(f"f{layer}_scores{i}{h}", [P, 2, 2 * P], F32)) for h in (0, 1)] for i in (0, 1)]
        bank = [ctx.enter_context(nc.psum_tensor(f"f{layer}_bank{i}", [P, 512], F32)) for i in range(3)]
        o_bank = ctx.enter_context(nc.psum_tensor(f"f{layer}_o_bank", [P, CHUNK], F32))
        y_banks = scores[0]

        steps = []
        for h in range(HALVES):
            for s in range(UNITS):
                n = h * UNITS + s
                steps.append(("scores", n))
                if s >= 4 and s % 2 == 0:
                    steps.append(("values", h * PAIRS + (s - 4) // 2))
                if s >= 2:
                    steps.append(("transpose", n - 2))
                steps += [("softmax", n), ("weigh", n)]
                if s == 2:
                    steps += [("load_x", h), ("load_tables", h)]
                if s == 4:
                    steps += [("load_x1", h), ("scale_tables", h)]
                if s == 6:
                    steps.append(("transpose_x", h))
            if h == 0:
                steps.append(("shift_keys", h))
            u0, p0, t0 = h * UNITS, h * PAIRS, h * TILES
            steps += [("project_qk", t0), ("project_qk", t0 + 1), ("values", p0 + 2), ("transpose", u0 + 6), ("transpose", u0 + 7),
                      ("rope", t0), ("values", p0 + 3), ("project_v", h), ("project_o", h), ("shift", h), ("rope", t0 + 1),
                      ("transpose_qk", t0), ("project_qk", t0 + 2), ("transpose_qk", t0 + 1), ("project_qk", t0 + 3), ("ln_stats", h),
                      ("rope", t0 + 2), ("ln_apply", h), ("transpose_h", h), ("x1_bias", h)]
            j0 = h * FH
            tail = {1: [("rope", t0 + 3)], 2: [("transpose_qk", t0 + 2)], 3: [("transpose_qk", t0 + 3)]}
            if attended is not None:
                tail[3].append(("add_attended", h))
            steps += [("up", j0)]
            for j in range(1, FH):
                steps += [("up", j0 + j), ("down", j0 + j - 1)] + tail.get(j, [])
            steps += [("down", j0 + FH - 1), ("out", h)]
        e, t0 = HALVES - 1, (HALVES - 1) * TILES
        before = [("load_x", e), ("load_tables", e), ("scale_tables", e), ("transpose_x", e), ("project_qk", t0), ("project_qk", t0 + 1),
                  ("project_v", e), ("rope", t0), ("rope", t0 + 1), ("transpose_qk", t0), ("project_qk", t0 + 2), ("transpose_qk", t0 + 1),
                  ("project_qk", t0 + 3), ("rope", t0 + 2), ("rope", t0 + 3), ("transpose_qk", t0 + 2), ("transpose_qk", t0 + 3)]

        def sem(name):
            return nc.alloc_semaphore(f"f{layer}_{name}")

        def count(name, sizes, unit=1, credit=0):
            return Count(sem(name), before, steps, sizes, unit, credit)

        fills = {"project_qk": 2, "project_v": TILES, "project_o": TILES, "transpose": 2, "transpose_x": CT, "transpose_h": CT,
                 "transpose_qk": 2, "up": 2}
        highs = {kind: n for kind, n in fills.items() if kind not in ("project_qk", "project_o", "up")}
        filled = count("filled", fills)
        hi_taken = count("hi_taken", highs)
        emptied = count("emptied", fills)
        scored = count("scored", {"scores": 1})
        maxed = count("maxed", {"scores": 2})
        negated = count("negated", {"scores": 2})
        exped = count("exped", {"scores": 2}, credit=1)
        weighed = count("weighed", {"weigh": 2})
        normalized = count("normalized", {"weigh": 2})
        o_filled = count("o_filled", {"values": 1})
        o_hi_taken = count("o_hi_taken", {"values": 1})
        o_emptied = count("o_emptied", {"values": 1}, credit=1)
        x_loaded = count("x_loaded", {"load_x": 1}, unit=32)
        tables_loaded = count("tables_loaded", {"load_tables": 1}, unit=16)
        tables_ready = count("tables_ready", {"scale_tables": 1})
        x1_loaded = count("x1_loaded", {"load_x1": 1}, unit=16)
        keys_shifted = count("keys_shifted", {"shift_keys": 1}, unit=16)
        raw_taken = count("raw_taken", {"project_qk": 2})
        clamped = count("clamped", {"project_qk": 1})
        norm_ready = count("norm_ready", {"project_qk": 1})
        cos_ready = count("cos_ready", {"rope": 1})
        sin_ready = count("sin_ready", {"rope": 1})
        rope_added = count("rope_added", {"rope": 1})
        roped = count("roped", {"rope": 1})
        shifted = count("shifted", {"shift": 1}, unit=48)
        edge_kept = count("edge_kept", {"shift_keys": 1}, unit=16)
        bn_done = count("bn_done", {"ln_stats": 1})
        aggregated = count("aggregated", {"ln_stats": 1})
        var_ready = count("var_ready", {"ln_stats": 1})
        rstd_ready = count("rstd_ready", {"ln_stats": 1})
        ln_scaled = count("ln_scaled", {"ln_apply": 1})
        ln_ready = count("ln_ready", {"ln_apply": 1})
        x1_biased = count("x1_biased", {"x1_bias": 1})
        attended_loaded = count("attended_loaded", {"add_attended": 1}, unit=16)
        attended_added = count("attended_added", {"add_attended": 1}, credit=1)
        gelued = count("gelued", {"up": 1})
        u_hi = count("u_hi", {"up": 1})
        u_ready = count("u_ready", {"up": 1})
        downed = count("downed", {"down": 1})
        x2_ready = count("x2_ready", {"out": 2}, credit=1)
        x2_stored = count("x2_stored", {"out": 1}, unit=16, credit=1)
        consts_loaded = sem("consts_loaded")
        staged = [sem(f"staged{i}") for i in (0, 1)]
        stage_hi_taken = sem("stage_hi_taken")
        stage_emptied = sem("stage_emptied")
        dve_carried, sp_carried = sem("dve_carried"), sem("sp_carried")
        zeroed = sem("zeroed")

        pieces = []
        for c in range(CT):
            rows = slice(c * P, (c + 1) * P)
            for c0, c1 in ((0, 2 * F_INNER), (2 * F_INNER, 3 * F_INNER)):
                pieces.append((wqkv_in[rows, c0:c1], wqkv[:, HI, c, c0:c1], wqkv[:, LO, c, c0:c1]))
        pieces.append((wo_in.rearrange("(c p) n -> p c n", p=P), wo[:, HI], wo[:, LO]))
        for c in range(CT):
            rows = slice(c * P, (c + 1) * P)
            for c0, c1 in ((0, HID), (HID, 2 * HID)):
                pieces.append((w1_in[rows, c0:c1], w1[:, HI, c, c0:c1], w1[:, LO, c, c0:c1]))
        for j0, j1, m in ((0, 4, HT), (4, FH - 1, HT), (FH - 1, FH, HL)):
            r0 = j0 * HT
            pieces.append((w2_in[r0:r0 + (j1 - j0) * m, :].rearrange("(j p) n -> p j n", p=m), w2[0:m, HI, j0:j1, :], w2[0:m, LO, j0:j1, :]))

        def stage_of(i):
            shape = pieces[i][1].shape
            if len(shape) == 2:
                return stage[:, i % 2, 0:shape[1]]
            return stage[0:shape[0], i % 2, 0:shape[1] * shape[2]].rearrange("p (c n) -> p c n", n=shape[2])

        def prepared(it, h):
            return 0 if it is None else (it + (h + 1) // HALVES) % BATCH, (h + 1) % HALVES

        def values_of(half, tile):
            return v_kept[:] if tile < 0 or (half == 0 and tile == TILES - 1) else v[:, tile]

        def value_operand(half, tile, part, pair, head):
            return values_of(half, tile)[:, part, pair, head:head + 2, :].rearrange("p b d -> p (b d)")

        def like(source, place):
            if len(place.shape) == 2:
                return source[:]
            if len(place.shape) == 3:
                return source[:].rearrange("p (a d) -> p a d", a=place.shape[1])
            return source[:].rearrange("p (a b d) -> p a b d", a=place.shape[1], b=place.shape[2])

        def by_head(a):
            return a.rearrange("p i (h d) -> p i h d", d=DH)

        def table(kind, tile):
            return tables[:, :, kind, tile, :].unsqueeze(2).broadcast_to([P, 2, F_HEADS, DH])

        def hidden_of(a):
            j = a % FH
            return j, HL if j == FH - 1 else HT

        def places_of(kind, a):
            if kind == "project_v":
                half = (a + 1) % HALVES
                return [(lambda part, t=t: values_of(half, t)[:, part, :, VALUE:VALUE_2 + 1:2, :]) for t in range(TILES)]
            if kind == "transpose":
                return [(lambda part, head=head: probT[:, part, head, a % 2 * 4 * P:(a % 2 + 1) * 4 * P]) for head in (0, 1)]
            if kind == "transpose_qk":
                col = a % TILES * P
                return [lambda part: q_o[:, part, :, col:col + P], lambda part: kT[:, part, :, P + col:2 * P + col]]
            assert kind in ("transpose_x", "transpose_h")
            return [(lambda part, c=c: actT[:, part, c, :]) for c in range(CT)]

        CONSTS = 15
        block = ctx.enter_context(nc.Block())

        @block.sync
        def _(sp):
            sp.sem_inc(x2_stored.sem, 1)
            sp.sem_inc(attended_added.sem, 1)

            def load_x(it, h):
                if it is not None:
                    if attended is None or h == 0:
                        sp.wait_ge(filled.sem, filled.past(it, ("transpose_h", h - 1), CT - 1) if h else filled.upto(it, -1))
                    if attended is not None:
                        sp.wait_ge(attended_added.sem, attended_added.upto(it, h - 1))
                sequence, half = prepared(it, h)
                sp.dma_start(x_tok[:, :, 0:P], tokens_of(state_in, sequence, half, ahead=1)[:, :, 0:P]).then_inc(x_loaded.sem, 16)
                sp.dma_start(x_tok[:, :, P:D], tokens_of(state_in, sequence, half, ahead=0)[:, :, P:D]).then_inc(x_loaded.sem, 16)

            def load_tables(it, h):
                if it is not None:
                    sp.wait_ge(roped.sem, roped.upto(it, h * TILES - 1))
                sp.dma_start(tables[:], tables_in[(h + 1) % HALVES]).then_inc(tables_loaded.sem, 16)

            load_x(None, HALVES - 1)
            load_tables(None, HALVES - 1)
            sp.dma_start(ident[:], identity).then_inc(consts_loaded, 16)
            for which, row in ((QUERY, q_scale), (KEY, k_scale)):
                row = row.unsqueeze(0).broadcast_to([P, DH])
                sp.dma_start(scale_rows[:, which, COS, :], row).then_inc(consts_loaded, 16)
                sp.dma_start(scale_rows[:, which, SIN, 0:DH // 2], row[:, DH // 2:DH]).then_inc(consts_loaded, 16)
                sp.dma_start(scale_rows[:, which, SIN, DH // 2:DH], row[:, 0:DH // 2]).then_inc(consts_loaded, 16)
            sp.dma_start(mask[:], masks.rearrange("s p k -> p s k")).then_inc(consts_loaded, 16)
            for row, place in ((ln_g, ln_g_row), (ln_b, ln_b_row), (b2, b2_row)):
                sp.dma_start(place[:], row.unsqueeze(0).broadcast_to([P, D])).then_inc(consts_loaded, 16)
            for which in (0, 1):
                c0, c1 = which * HID, which * HID + (FH - 1) * HT
                sp.dma_start(b1_cols[0:HT, which, 0:FH - 1], b1[c0:c1].rearrange("(j p) -> p j", p=HT), allow_slow_non_contiguous=True).then_inc(consts_loaded, 16)
                sp.dma_start(b1_cols[0:HL, which, FH - 1:FH], b1[c1:c0 + HID].rearrange("(j p) -> p j", p=HL), allow_slow_non_contiguous=True).then_inc(consts_loaded, 16)
            for i, (src, _, _) in enumerate(pieces):
                if i >= 2:
                    sp.wait_ge(stage_emptied, i - 1)
                sp.dma_start(stage_of(i), src).then_inc(staged[i % 2], 16)
            sp.wait_ge(zeroed, 1)
            with sp.Fori(0, BATCH) as it:
                for kind, a in steps:
                    if kind == "load_x":
                        load_x(it, a)
                    elif kind == "load_tables":
                        load_tables(it, a)
                    elif kind == "load_x1":
                        sp.wait_ge(x2_stored.sem, x2_stored.upto(it, a - 1))
                        sp.sem_inc(sp_carried, 1)
                        sp.dma_start(x1[:], tokens_of(state_in, it, a, ahead=1)).then_inc(x1_loaded.sem, 16)
                    elif kind == "shift_keys":
                        sp.wait_ge(scored.sem, scored.past(it, ("scores", (a + 1) * UNITS - 1)))
                        sp.dma_start(kT[:, :, :, 0:P].bitcast(F32), kT[:, :, :, CHUNK:CHUNK + P].bitcast(F32)).then_inc(keys_shifted.sem, 16)
                    elif kind == "shift":
                        sp.wait_ge(emptied.sem, emptied.past(it, ("project_o", a), TILES - 1))
                        sp.dma_start(x_tok[1:P, :, P:D], x1[0:P - 1, :, P:D]).then_inc(shifted.sem, 16)
                        sp.dma_start(x_tok[0:1, 1:TILES, P:D], x1[P - 1:P, 0:TILES - 1, P:D]).then_inc(shifted.sem, 16)
                        if a:
                            sp.wait_ge(edge_kept.sem, edge_kept.past(it, ("shift_keys", 0)))
                        sp.dma_start(x_tok[0:1, 0, P:D], edge[:, a, :]).then_inc(shifted.sem, 16)
                        if a == 0:
                            sp.dma_start(edge[:, 1, :], x1[P - 1:P, TILES - 1, P:D]).then_inc(edge_kept.sem, 16)
                    elif kind == "add_attended":
                        sp.wait_ge(filled.sem, filled.past(it, ("transpose_h", a), CT - 1))
                        sp.dma_start(x_tok[:], tokens_of(attended, it, a)).then_inc(attended_loaded.sem, 16)
                    elif kind == "out":
                        sp.wait_ge(x2_ready.sem, x2_ready.past(it, (kind, a), 1))
                        sp.dma_start(tokens_of(state_out, it, a, ahead=ahead_out), x1[:]).then_inc(x2_stored.sem, 16)
            sp.wait_ge(x2_stored.sem, x2_stored.upto(BATCH, -1))

        @block.gpsimd
        def _(pool):
            pool.memset(minus_half[:], -0.5)
            pool.memset(edge[:], 0.0)
            pool.memset(kT[:, :, :, 0:P].bitcast(F32), 0.0)
            for t in range(TILES):
                for part in (HI, LO):
                    pool.memset(v[:, t, part, :, ZERO, :].bitcast(F32), 0.0)
            for part in (HI, LO):
                last = pool.memset(v_kept[:, part, :, ZERO, :].bitcast(F32), 0.0)
            last.then_inc(zeroed, 1)
            pool.wait_ge(zeroed, 1)

            def scale_tables(it, h):
                pool.wait_ge(tables_loaded.sem, tables_loaded.past(it, ("load_tables", h)))
                for which in (QUERY, KEY):
                    last = nc.gpsimd.tensor_tensor(tables[:, which], tables[:, which],
                                                   scale_rows[:, which].unsqueeze(2).broadcast_to([P, 2, TILES, DH]), ALU.mult)
                last.then_inc(tables_ready.sem, 1)

            def norms(it, a):
                pool.wait_ge(clamped.sem, clamped.past(it, ("project_qk", a)))
                n = norm[:, a % 2].rearrange("p i h -> p (i h)")
                nc.gpsimd.tensor_tensor(n, n, minus_half[:], ALU.pow).then_inc(norm_ready.sem, 1)

            def rope(it, a):
                n = roped.number(it, ("rope", a))
                pool.wait_ge(raw_taken.sem, raw_taken.past(it, ("project_qk", a), 1))
                if it is not None or n >= 1:
                    pool.wait_ge(roped.sem, roped.upto(it, n - 1))
                for which in (QUERY, KEY):
                    last = nc.gpsimd.tensor_tensor(by_head(cos_part[:])[:, which], by_head(qk_tok[:, a % 2])[:, which],
                                                   table(COS, a % TILES)[:, which], ALU.mult)
                last.then_inc(cos_ready.sem, 1)
                pool.wait_ge(cos_ready.sem, cos_ready.past(it, ("rope", a)))
                pool.wait_ge(sin_ready.sem, sin_ready.past(it, ("rope", a)))
                nc.gpsimd.tensor_tensor(cos_part[:], cos_part[:], sin_part[:], ALU.add).then_inc(rope_added.sem, 1)

            pool.wait_ge(consts_loaded, 16 * CONSTS)
            for kind, a in before:
                if kind == "scale_tables":
                    scale_tables(None, a)
                elif kind == "project_qk":
                    norms(None, a)
                elif kind == "rope":
                    if a % TILES == 0:
                        pool.wait_ge(tables_ready.sem, tables_ready.past(None, ("scale_tables", a // TILES)))
                    rope(None, a)
            with pool.Fori(0, BATCH) as it:
                for kind, a in steps:
                    if kind == "weigh":
                        for head in (0, 1):
                            pool.wait_ge(weighed.sem, weighed.past(it, (kind, a), head))
                            part = prob[:, a % 2, head]
                            nc.gpsimd.tensor_tensor(part, part, weight[:, a % 2, head].unsqueeze(2).broadcast_to([P, 2, 2 * P]),
                                                    ALU.mult).then_inc(normalized.sem, 1)
                    elif kind == "scale_tables":
                        scale_tables(it, a)
                    elif kind == "project_qk":
                        norms(it, a)
                    elif kind == "rope":
                        if a % TILES == 0:
                            pool.wait_ge(tables_ready.sem, tables_ready.past(it, ("scale_tables", a // TILES)))
                        rope(it, a)
                    elif kind == "ln_stats":
                        pool.wait_ge(var_ready.sem, var_ready.past(it, (kind, a)))
                        nc.gpsimd.tensor_tensor(rstd[:], rstd[:], minus_half[:, 0:TILES], ALU.pow).then_inc(rstd_ready.sem, 1)
                    elif kind == "x1_bias":
                        pool.wait_ge(ln_scaled.sem, ln_scaled.past(it, ("ln_apply", a)))
                        if a == 0:
                            pool.wait_ge(edge_kept.sem, edge_kept.past(it, ("shift_keys", 0)))
                        nc.gpsimd.tensor_tensor(x1[:], x1[:], b2_row[:].unsqueeze(1).broadcast_to([P, TILES, D]), ALU.add).then_inc(x1_biased.sem, 1)
                    elif kind == "add_attended":
                        pool.wait_ge(attended_loaded.sem, attended_loaded.past(it, (kind, a)))
                        pool.wait_ge(x1_biased.sem, x1_biased.past(it, ("x1_bias", a)))
                        nc.gpsimd.tensor_tensor(x1[:], x1[:], x_tok[:], ALU.add).then_inc(attended_added.sem, 1)
                    elif kind == "up":
                        _, m = hidden_of(a)
                        pool.wait_ge(u_hi.sem, u_hi.past(it, (kind, a)))
                        nc.gpsimd.tensor_tensor(u[0:m, a % 4, LO, :], gu[0:m, a % 2, :], u[0:m, a % 4, HI, :].bitcast(F32),
                                                ALU.subtract).then_inc(u_ready.sem, 1)

        @block.tensor
        def _(pe):
            def take_bank(it, n):
                if n >= 3 or it is not None:
                    pe.wait_ge(emptied.sem, emptied.upto(it, n - 3 if n >= 3 else -1))
                return bank[n % 3]

            def products(out, lhs, rhs, tiles):
                order = [(c, a, b) for c in range(tiles) for a, b in PASSES]
                for i, (c, a, b) in enumerate(order):
                    last = nc.tensor.matmul(out, lhs(c, a), rhs(c, b), start=(i == 0), stop=(i == len(order) - 1))
                return last

            def transpose_tok(it, kind, h, source):
                for c in range(CT):
                    out = take_bank(it, filled.number(it, (kind, h), c))
                    for t in range(TILES):
                        last = nc.tensor.transpose(out[:, t * P:(t + 1) * P], source[:, t, c * P:(c + 1) * P], ident[:])
                    last.then_inc(filled.sem, 1)

            def prepare(it, kind, a):
                if kind == "transpose_x":
                    pe.wait_ge(x_loaded.sem, x_loaded.past(it, ("load_x", a)))
                    transpose_tok(it, kind, a, x_tok)
                elif kind == "project_qk":
                    if a % TILES == 0:
                        pe.wait_ge(emptied.sem, emptied.past(it, ("transpose_x", a // TILES), CT - 1))
                    for which in (QUERY, KEY):
                        out = take_bank(it, filled.number(it, (kind, a), which))
                        t = a % TILES
                        products(out[:], lambda c, part: actT[:, part, c, t * P:(t + 1) * P],
                                 lambda c, part: wqkv[:, part, c, which * F_INNER:(which + 1) * F_INNER], CT).then_inc(filled.sem, 1)
                elif kind == "project_v":
                    for t in range(TILES):
                        out = take_bank(it, filled.number(it, (kind, a), t))
                        products(out[:], lambda c, part: actT[:, part, c, t * P:(t + 1) * P],
                                 lambda c, part: wqkv[:, part, c, 2 * F_INNER:3 * F_INNER], CT).then_inc(filled.sem, 1)
                elif kind == "transpose_qk":
                    pe.wait_ge(roped.sem, roped.past(it, ("rope", a)))
                    for which in (QUERY, KEY):
                        out = take_bank(it, filled.number(it, (kind, a), which))
                        for pair in range(PAIRS):
                            last = nc.tensor.transpose(out[:, pair * P:(pair + 1) * P], qk_tok[:, a % 2, which, pair * P:(pair + 1) * P], ident[:])
                        last.then_inc(filled.sem, 1)

            pe.wait_ge(consts_loaded, 16 * CONSTS)
            for kind, a in before:
                if kind == "project_qk" and a % TILES == 0:
                    pe.wait_ge(stage_emptied, len(pieces))
                prepare(None, kind, a)
            pe.wait_ge(zeroed, 1)
            with pe.Fori(0, BATCH) as it:
                for kind, a in steps:
                    prepare(it, kind, a)
                    if kind == "scores":
                        half, s = divmod(a, UNITS)
                        pair, tile = s // 2, 2 * (s % 2)
                        if s == 0:
                            pe.wait_ge(emptied.sem, emptied.past(it, ("transpose_qk", half * TILES - 1), 1) if half else emptied.upto(it, -1))
                            if half:
                                pe.wait_ge(keys_shifted.sem, keys_shifted.past(it, ("shift_keys", 0)))
                            pe.wait_ge(x2_ready.sem, x2_ready.upto(it, 2 * half - 1))
                        pe.wait_ge(exped.sem, exped.past(it, ("scores", a - 2), 1) if a >= 2 else exped.upto(it, -1))
                        for t in (0, 1):
                            col = (tile + t) * P
                            for i, (qp, kp) in enumerate(PASSES):
                                for head in (0, 1):
                                    rows = slice(DH * head, DH * (head + 1))
                                    mm = nc.tensor.matmul(scores[a % 2][head][:, t, :], q_o[rows, qp, pair, col:col + P],
                                                          kT[rows, kp, pair, col:col + 2 * P], start=(i == 0), stop=(i == 2))
                        mm.then_inc(scored.sem, 1)
                    elif kind == "transpose":
                        for head in (0, 1):
                            out = take_bank(it, filled.number(it, (kind, a), head))
                            pe.wait_ge(normalized.sem, normalized.past(it, ("weigh", a), head))
                            for j in range(4):
                                last = nc.tensor.transpose(out[:, j * P:(j + 1) * P], prob[:, a % 2, head, j // 2, (j % 2) * P:(j % 2 + 1) * P],
                                                           ident[:])
                            last.then_inc(filled.sem, 1)
                    elif kind == "values":
                        half, pair = divmod(a, PAIRS)
                        pe.wait_ge(emptied.sem, emptied.past(it, ("transpose", 2 * a + 1), 1))
                        pe.wait_ge(o_emptied.sem, o_emptied.upto(it, a - 1))
                        order = [(kt, head, vp, pp) for kt in key_tiles(half) for head in (0, 1) for vp, pp in PASSES]
                        for i, ((tile, p0, p1, o0, o1), head, vp, pp) in enumerate(order):
                            mm = nc.tensor.matmul(o_bank[:, o0:o1], value_operand(half, tile, vp, pair, head),
                                                  probT[:, pp, head, p0:p1], start=(i == 0), stop=(i == len(order) - 1),
                                                  skip_group_check=True)
                        mm.then_inc(o_filled.sem, 1)
                    elif kind == "project_o":
                        pe.wait_ge(o_emptied.sem, o_emptied.past(it, ("values", PAIRS * (a + 1) - 1)))
                        for t in range(TILES):
                            out = take_bank(it, filled.number(it, (kind, a), t))
                            products(out[:, 0:D], lambda c, part: q_o[:, part, c, t * P:(t + 1) * P],
                                     lambda c, part: wo[:, part, c, :], PAIRS).then_inc(filled.sem, 1)
                    elif kind == "transpose_h":
                        pe.wait_ge(ln_ready.sem, ln_ready.past(it, ("ln_apply", a)))
                        transpose_tok(it, kind, a, x_tok)
                    elif kind == "up":
                        j, m = hidden_of(a)
                        if j == 0:
                            pe.wait_ge(emptied.sem, emptied.past(it, ("transpose_h", a // FH), CT - 1))
                        for i, c0 in enumerate((HID, 0)):
                            out = take_bank(it, filled.number(it, (kind, a), i))
                            col = c0 + j * HT
                            products(out[0:m, :], lambda c, part: w1[:, part, c, col:col + m], lambda c, part: actT[:, part, c, :],
                                     CT).then_inc(filled.sem, 1)
                    elif kind == "down":
                        j, m = hidden_of(a)
                        pe.wait_ge(u_ready.sem, u_ready.past(it, ("up", a)))
                        if j == 0:
                            pe.wait_ge(exped.sem, exped.past(it, ("scores", (a // FH + 1) * UNITS - 1), 1))
                        for t in range(TILES):
                            for i, (up, wp) in enumerate(PASSES):
                                mm = nc.tensor.matmul(y_banks[t // 2][:, t % 2, :], u[0:m, a % 4, up, t * P:(t + 1) * P], w2[0:m, wp, j, :],
                                                      start=(j == 0 and t % 2 == 0 and i == 0), stop=(j == FH - 1 and t % 2 == 1 and i == 2),
                                                      skip_group_check=True)
                        mm.then_inc(downed.sem, 1)

        @block.scalar
        def _(act):
            act.sem_inc(exped.sem, 1)
            for i, (_, hi, _) in enumerate(pieces):
                act.wait_ge(staged[i % 2], 16 * (i // 2 + 1))
                nc.scalar.activation(hi, stage_of(i), ACT.Copy).then_inc(stage_hi_taken, 1)

            def take_high(it, kind, a):
                for i, place in enumerate(places_of(kind, a)):
                    n = filled.number(it, (kind, a), i)
                    act.wait_ge(filled.sem, filled.upto(it, n))
                    nc.scalar.activation(place(HI), like(bank[n % 3], place(HI)), ACT.Copy).then_inc(hi_taken.sem, 1)

            def take_raw(it, a):
                first = filled.number(it, ("project_qk", a))
                if ("transpose_qk", a - 2) in (filled.first0 if it is None else filled.first):
                    act.wait_ge(filled.sem, filled.past(it, ("transpose_qk", a - 2), 1))
                elif it is not None:
                    act.wait_ge(filled.sem, filled.upto(it, -1))
                for which in (QUERY, KEY):
                    act.wait_ge(filled.sem, filled.upto(it, first + which))
                    nc.scalar.activation(qk_tok[:, a % 2, which, :], bank[(first + which) % 3][:], ACT.Copy)
                    if ("project_qk", a - 1) in (emptied.first0 if it is None else emptied.first):
                        act.wait_ge(emptied.sem, emptied.past(it, ("project_qk", a - 1), which))
                    elif it is not None:
                        act.wait_ge(emptied.sem, emptied.upto(it, -1))
                    nc.scalar.activation(square[:, which, :], bank[(first + which) % 3][:], ACT.Square).then_inc(raw_taken.sem, 1)

            for kind, a in before:
                if kind in highs:
                    take_high(None, kind, a)
                elif kind == "project_qk":
                    take_raw(None, a)
            with act.Fori(0, BATCH) as it:
                for kind, a in steps:
                    if kind == "transpose_qk" and a == TILES - 1:
                        act.wait_ge(keys_shifted.sem, keys_shifted.past(it, ("shift_keys", 0)))
                    if kind in highs:
                        take_high(it, kind, a)
                    elif kind == "project_qk":
                        take_raw(it, a)
                    elif kind == "softmax":
                        for head in (0, 1):
                            act.wait_ge(negated.sem, negated.past(it, ("scores", a), head))
                            for t in (0, 1):
                                last = nc.scalar.activation(prob[:, a % 2, head, t, :], scores[a % 2][head][:, t, :], ACT.Exp,
                                                            bias=neg_max[:, a % 2, head, t:t + 1], accum_out=row_sum[:, a % 2, head, t:t + 1])
                            last.then_inc(exped.sem, 1)
                    elif kind == "values":
                        act.wait_ge(o_filled.sem, o_filled.past(it, (kind, a)))
                        nc.scalar.activation(q_o[:, HI, a % PAIRS, :], o_bank[:], ACT.Copy).then_inc(o_hi_taken.sem, 1)
                    elif kind == "up":
                        j, m = hidden_of(a)
                        n = filled.number(it, (kind, a), 0)
                        act.wait_ge(filled.sem, filled.upto(it, n))
                        if a >= 2:
                            act.wait_ge(u_ready.sem, u_ready.past(it, ("up", a - 2)))
                        nc.scalar.activation(gu[0:m, a % 2, :], bank[n % 3][0:m, :], ACT.Gelu, bias=b1_cols[0:m, 1, j:j + 1]).then_inc(gelued.sem, 1)
                        act.wait_ge(emptied.sem, emptied.past(it, (kind, a), 1))
                        if j >= 4:
                            act.wait_ge(downed.sem, downed.past(it, ("down", a - 4)))
                        nc.scalar.activation(u[0:m, a % 4, HI, :], gu[0:m, a % 2, :], ACT.Copy).then_inc(u_hi.sem, 1)

        @block.vector
        def _(dve):
            dve.sem_inc(o_emptied.sem, 1)
            dve.sem_inc(x2_ready.sem, 1)
            for i, (_, hi, lo) in enumerate(pieces):
                dve.wait_ge(stage_hi_taken, i + 1)
                nc.vector.tensor_tensor(lo, stage_of(i), hi.bitcast(F32), ALU.subtract).then_inc(stage_emptied, 1)

            def take_low(it, kind, a):
                for i, place in enumerate(places_of(kind, a)):
                    n = filled.number(it, (kind, a), i)
                    dve.wait_ge(hi_taken.sem, hi_taken.past(it, (kind, a), i))
                    nc.vector.tensor_tensor(place(LO), like(bank[n % 3], place(LO)), place(HI).bitcast(F32), ALU.subtract).then_inc(emptied.sem, 1)

            def sum_squares(it, a):
                for which in (QUERY, KEY):
                    dve.wait_ge(raw_taken.sem, raw_taken.past(it, ("project_qk", a), which))
                    nc.vector.tensor_reduce(norm[:, a % 2, which, :], square[:, which, :].rearrange("p (h d) -> p h d", d=DH), AXIS.X,
                                            ALU.add).then_inc(emptied.sem, 1)
                dve.wait_ge(emptied.sem, emptied.past(it, ("project_qk", a), KEY))
                nc.vector.tensor_scalar(norm[:, a % 2], norm[:, a % 2], 1e-24, None, ALU.max).then_inc(clamped.sem, 1)

            def rope(it, a):
                if a % TILES == 0:
                    dve.wait_ge(tables_ready.sem, tables_ready.past(it, ("scale_tables", a // TILES)))
                raw, sin, lower, upper = by_head(qk_tok[:, a % 2]), table(SIN, a % TILES), slice(0, DH // 2), slice(DH // 2, DH)
                nc.vector.tensor_tensor(by_head(sin_part[:])[:, :, :, lower], raw[:, :, :, upper], sin[:, :, :, lower], ALU.mult)
                nc.vector.tensor_tensor(by_head(sin_part[:])[:, :, :, upper], raw[:, :, :, lower], sin[:, :, :, upper],
                                        ALU.mult).then_inc(sin_ready.sem, 1)
                dve.wait_ge(rope_added.sem, rope_added.past(it, ("rope", a)))
                dve.wait_ge(norm_ready.sem, norm_ready.past(it, ("project_qk", a)))
                nc.vector.tensor_tensor(raw, by_head(cos_part[:]), norm[:, a % 2].unsqueeze(3).broadcast_to([P, 2, F_HEADS, DH]),
                                        ALU.mult).then_inc(roped.sem, 1)

            dve.wait_ge(consts_loaded, 16 * CONSTS)
            for kind, a in before:
                if kind in highs:
                    take_low(None, kind, a)
                elif kind == "project_qk":
                    sum_squares(None, a)
                elif kind == "rope":
                    rope(None, a)
            with dve.Fori(0, BATCH) as it:
                for kind, a in steps:
                    if kind == "scores":
                        half, s = divmod(a, UNITS)
                        tile = 2 * (s % 2)
                        dve.wait_ge(scored.sem, scored.past(it, (kind, a)))
                        dve.sem_inc(dve_carried, 1)
                        for head in (0, 1):
                            for t in (0, 1):
                                sc = scores[a % 2][head][:, t, :]
                                last = nc.vector.tensor_tensor_reduce(out=sc, in0=sc, in1=mask[:, min(half * TILES + tile + t, 1)], scale=1.0,
                                                                      scalar=-3e38, op0=ALU.add, op1=ALU.max,
                                                                      accum_out=row_max[:, a % 2, head, t:t + 1])
                            last.then_inc(maxed.sem, 1)
                            dve.wait_ge(maxed.sem, maxed.past(it, (kind, a), head))
                            nc.vector.tensor_scalar(neg_max[:, a % 2, head], row_max[:, a % 2, head], -1.0, None, ALU.mult).then_inc(negated.sem, 1)
                    elif kind in highs:
                        take_low(it, kind, a)
                    elif kind == "weigh":
                        for head in (0, 1):
                            dve.wait_ge(exped.sem, exped.past(it, ("scores", a), head))
                            nc.vector.reciprocal(weight[:, a % 2, head], row_sum[:, a % 2, head]).then_inc(weighed.sem, 1)
                    elif kind == "values":
                        dve.wait_ge(o_hi_taken.sem, o_hi_taken.past(it, (kind, a)))
                        nc.vector.tensor_tensor(q_o[:, LO, a % PAIRS, :], o_bank[:], q_o[:, HI, a % PAIRS, :].bitcast(F32),
                                                ALU.subtract).then_inc(o_emptied.sem, 1)
                    elif kind == "project_qk":
                        sum_squares(it, a)
                    elif kind == "rope":
                        rope(it, a)
                    elif kind == "project_o":
                        dve.wait_ge(x1_loaded.sem, x1_loaded.past(it, ("load_x1", a)))
                        for t in range(TILES):
                            n = filled.number(it, (kind, a), t)
                            dve.wait_ge(filled.sem, filled.upto(it, n))
                            nc.vector.tensor_tensor(x1[:, t, :], bank[n % 3][:, 0:D], x1[:, t, :], ALU.add).then_inc(emptied.sem, 1)
                    elif kind == "ln_stats":
                        dve.wait_ge(emptied.sem, emptied.past(it, ("project_o", a), TILES - 1))
                        dve.wait_ge(shifted.sem, shifted.past(it, ("shift", a)))
                        for t in range(TILES):
                            nc.vector.bn_stats(bn[:, t, 0, :], x1[:, t, 0:P])
                            last = nc.vector.bn_stats(bn[:, t, 1, :], x_tok[:, t, P:D])
                        last.then_inc(bn_done.sem, 1)
                        dve.wait_ge(bn_done.sem, bn_done.past(it, (kind, a)))
                        dve.sem_inc(dve_carried, 1)
                        for t in range(TILES):
                            last = nc.vector.bn_aggr(mean_var[:, t, :], bn[:, t])
                        last.then_inc(aggregated.sem, 1)
                        dve.wait_ge(aggregated.sem, aggregated.past(it, (kind, a)))
                        nc.vector.tensor_scalar(rstd[:], mean_var[:, :, 1], 1e-5, None, ALU.add).then_inc(var_ready.sem, 1)
                    elif kind == "ln_apply":
                        for t in range(TILES):
                            for source, cols in ((x1, slice(0, P)), (x_tok, slice(P, D))):
                                last = nc.vector.scalar_tensor_tensor(out=x_tok[:, t, cols], in0=source[:, t, cols], scalar=mean_var[:, t, 0:1],
                                                                      in1=ln_g_row[:, cols], op0=ALU.subtract, op1=ALU.mult)
                        last.then_inc(ln_scaled.sem, 1)
                        dve.wait_ge(ln_scaled.sem, ln_scaled.past(it, (kind, a)))
                        dve.wait_ge(rstd_ready.sem, rstd_ready.past(it, ("ln_stats", a)))
                        for t in range(TILES):
                            last = nc.vector.scalar_tensor_tensor(out=x_tok[:, t, :], in0=x_tok[:, t, :], scalar=rstd[:, t:t + 1], in1=ln_b_row[:],
                                                                  op0=ALU.mult, op1=ALU.add)
                        last.then_inc(ln_ready.sem, 1)
                    elif kind == "up":
                        j, m = hidden_of(a)
                        dve.wait_ge(gelued.sem, gelued.past(it, (kind, a)))
                        n = filled.number(it, (kind, a), 1)
                        dve.wait_ge(filled.sem, filled.upto(it, n))
                        nc.vector.scalar_tensor_tensor(out=gu[0:m, a % 2, :], in0=bank[n % 3][0:m, :], scalar=b1_cols[0:m, 0, j:j + 1],
                                                       in1=gu[0:m, a % 2, :], op0=ALU.add, op1=ALU.mult).then_inc(emptied.sem, 2)
                    elif kind == "out":
                        last_step = ("add_attended", a) if attended is not None else ("x1_bias", a)
                        done = attended_added if attended is not None else x1_biased
                        dve.wait_ge(downed.sem, downed.past(it, ("down", (a + 1) * FH - 1)))
                        dve.wait_ge(done.sem, done.past(it, last_step))
                        for i in (0, 1):
                            nc.vector.tensor_tensor(x1[:, 2 * i:2 * i + 2, :], y_banks[i][:], x1[:, 2 * i:2 * i + 2, :],
                                                    ALU.add).then_inc(x2_ready.sem, 1)


def local_attention_program(nc, x, gamma, w_qkv, w_gates, b_gates, w_out, wqkv, q_scale, k_scale, wo, ln_g, ln_b, w1, b1, w2, b2,
                            gated_masks, layer_masks, identity, tables, out):
    normed = nc.dram_tensor("normed", [BATCH, SEQ + 1, D], F32).ap()
    hidden = nc.dram_tensor("hidden", [BATCH, SEQ + 1, D], F32).ap()
    attended = nc.dram_tensor("attended", [BATCH, SEQ, D], F32).ap()
    attention_phase(nc, x, gamma, w_qkv, w_gates, b_gates, w_out, gated_masks, identity, normed, hidden, attended)
    weights = (wqkv, q_scale, k_scale, wo, ln_g, ln_b, w1, b1, w2, b2)
    ffn_phase(nc, 0, normed, hidden, 1, None, *[w[0] for w in weights], layer_masks, identity, tables)
    ffn_phase(nc, 1, hidden, out, 0, attended, *[w[1] for w in weights], layer_masks, identity, tables)


def window_masks(window):
    query, key = np.arange(P)[:, None], np.arange(2 * P)[None]
    distance = P + query - key
    other = np.where((distance >= 0) & (distance <= window), 0.0, MASKED)
    first = np.where(key < P, MASKED, other)
    return np.stack([first, other]).astype(np.float32)


def rotary_tables():
    f = np.float32
    half_idx = np.arange(0, DH, 2, dtype=f)
    inv_freq = f(1) / f(10000) ** (half_idx / f(DH))
    t = np.arange(SEQ, dtype=f)
    freqs = t[:, None] * inv_freq[None, :]
    base = (half_idx + f(0.4 * DH)) / f(1.4 * DH)
    scale = base[None, :] ** ((t - SEQ // 2) / f(F_WINDOW // 2))[:, None]
    freqs, scale = (np.concatenate([a, a], axis=-1) for a in (freqs, scale))
    sign = np.where(np.arange(DH) < DH // 2, f(-1), f(1))
    cos, sin = np.cos(freqs), np.sin(freqs) * sign
    tables = np.stack([f(8) * cos * scale, f(8) * sin * scale, cos / scale, sin / scale], axis=1)
    return tables.reshape(HALVES, TILES, P, 2, 2, DH).transpose(0, 2, 3, 4, 1, 5).astype(f)


def kernel(L0_attn_x, L0_attn_gamma, L0_attn_W_qkv, L0_attn_W_gates, L0_attn_b_gates, L0_attn_W_out, L0_ffn_wqkv, L0_ffn_q_scale,
           L0_ffn_k_scale, L0_ffn_wo, L0_ffn_ln_g, L0_ffn_ln_b, L0_ffn_w1, L0_ffn_b1, L0_ffn_w2, L0_ffn_b2):
    import concourse.bacc as bacc
    from concourse.bass_utils import run_bass_kernel_spmd

    arrays = {
        "x": L0_attn_x, "gamma": L0_attn_gamma, "w_qkv": L0_attn_W_qkv, "w_gates": L0_attn_W_gates, "b_gates": L0_attn_b_gates,
        "w_out": L0_attn_W_out, "wqkv": L0_ffn_wqkv, "q_scale": L0_ffn_q_scale, "k_scale": L0_ffn_k_scale, "wo": L0_ffn_wo,
        "ln_g": L0_ffn_ln_g, "ln_b": L0_ffn_ln_b, "w1": L0_ffn_w1, "b1": L0_ffn_b1, "w2": L0_ffn_w2, "b2": L0_ffn_b2,
        "gated_masks": window_masks(A_WINDOW), "layer_masks": window_masks(F_WINDOW), "identity": np.eye(P, dtype=np.float32),
        "tables": rotary_tables()}
    arrays = {f"in_{name}": np.ascontiguousarray(a) for name, a in arrays.items()}
    nc = bacc.Bacc("TRN2", target_bir_lowering=False, num_devices=1)
    args = [nc.dram_tensor(name, a.shape, mybir.dt.from_np(a.dtype), kind="ExternalInput").ap() for name, a in arrays.items()]
    out = nc.dram_tensor("out", (BATCH, SEQ, D), F32, kind="ExternalOutput").ap()
    local_attention_program(nc, *args, out)
    return run_bass_kernel_spmd(nc, [arrays], core_ids=[0]).results[0]["out"]
```

```python
from contextlib import ExitStack

import numpy as np
from concourse import mybir

F32 = mybir.dt.float32
F32R = mybir.dt.float32r
ALU = mybir.AluOpType
ACT = mybir.ActivationFunctionType
AXIS = mybir.AxisListType

P = 128
D = 256
CT = D // P
DH = 64
SEQ = 1024
BATCH = 4
TILES = 4
CHUNK = TILES * P
HALVES = SEQ // CHUNK
CHUNKS = BATCH * HALVES
PAIRS = 4
GROUP = 2 * PAIRS
GC = GROUP * DH
UNITS = 2 * PAIRS
HI, LO = 0, 1
PASSES = ((HI, HI), (HI, LO), (LO, HI))
MASKED = -1e30
VALUE, ZERO, VALUE_2 = range(3)

A_HEADS, A_WINDOW = 16, 64
A_GROUPS = A_HEADS // GROUP
A_INNER = A_HEADS * DH


def numbered(steps, sizes):
    first, n = {}, 0
    for step in steps:
        if step[0] in sizes:
            first[step] = n
            n += sizes[step[0]]
    return first, n


class Count:

    def __init__(self, sem, before, steps, sizes, unit=1, credit=0):
        self.sem, self.unit, self.credit = sem, unit, credit
        self.first0, self.before = numbered(before, sizes)
        self.first, self.each = numbered(steps, sizes)

    def number(self, it, step, i=0):
        return (self.first0 if it is None else self.first)[step] + i

    def past(self, it, step, i=0):
        return self.upto(it, self.number(it, step, i))

    def upto(self, it, n):
        if it is None:
            return self.credit + self.unit * (n + 1)
        return it * (self.unit * self.each) + (self.credit + self.unit * (self.before + n + 1))


def key_tiles(half):
    for kt in range(-1 if half else 0, TILES):
        yield kt, max(2 * kt + 1, 0) * P, min(2 * kt + 3, 2 * TILES) * P, max(kt, 0) * P, min(kt + 2, TILES) * P


def tokens_of(state, sequence, half, ahead=0):
    return state[sequence, ahead + half * CHUNK:ahead + (half + 1) * CHUNK, :].rearrange("(t p) d -> p t d", p=P)


def attention_phase(nc, x, gamma, w_qkv, w_gates, b_gates, w_out, masks, identity, normed, hidden, attended):
    with ExitStack() as ctx:
        def sb(name, shape, dt=F32):
            return ctx.enter_context(nc.sbuf_tensor("a_" + name, shape, dt))

        BLOCKS = HALVES * A_GROUPS
        NU = BLOCKS * UNITS
        NP = BLOCKS * PAIRS
        K0 = P - A_WINDOW
        KEYS = A_WINDOW + P

        wqkv = sb("wqkv", [P, 2, CT, 3 * A_INNER], F32R)
        wout = sb("wout", [P, 2, A_INNER // P, D], F32R)
        wgate = sb("wgate", [P, 2, CT, A_HEADS], F32R)
        ident = sb("ident", [P, P])
        mask = sb("mask", [P, 2, KEYS])
        gamma_row = sb("gamma_row", [P, D])
        bgate_row = sb("bgate_row", [P, A_HEADS])
        zero_rows = sb("zero_rows", [BATCH, D])
        minus_half = sb("minus_half", [P, TILES])
        x_tok = sb("x_tok", [P, TILES, D])
        xT = sb("xT", [P, 2, CT, CHUNK], F32R)
        q_o = sb("q_o", [P, A_GROUPS, 2, PAIRS, CHUNK], F32R)
        kT = sb("kT", [P, 2, PAIRS, A_WINDOW + CHUNK], F32R)
        k_kept = sb("k_kept", [P, A_GROUPS, 2, PAIRS, A_WINDOW], F32R)
        v = sb("v", [P, TILES, 2, PAIRS, 3, DH], F32R)
        v_kept = sb("v_kept", [P, A_GROUPS, 2, PAIRS, 3, DH], F32R)
        probT = sb("probT", [P, 2, 2, 2 * TILES * P], F32R)
        prob = sb("prob", [P, 2, 2, 2, 2 * P])
        y_tok = sb("y_tok", [P, TILES, D])
        square = sb("square", [P, D], mybir.dt.bfloat16)
        bn = sb("bn", [P, TILES, 6])
        mean_var = sb("mean_var", [P, TILES, 2])
        rstd = sb("rstd", [P, TILES])
        sumsq = sb("sumsq", [P, TILES])
        rms = sb("rms", [P, TILES])
        gate_in = sb("gate_in", [P, TILES, A_HEADS])
        gate = sb("gate", [P, HALVES, TILES, A_HEADS])
        row_max = sb("row_max", [P, 2, 2, 2])
        neg_max = sb("neg_max", [P, 2, 2, 2])
        row_sum = sb("row_sum", [P, 2, 2, 2])
        row_inv = sb("row_inv", [P, 2, 2, 2])
        weight = sb("weight", [P, 2, 2, 2])
        halves = prob[:].rearrange("p a b c d -> p (a b c d)").rearrange("p (s n) -> p s n", s=2)
        stages = [halves[:, 0], halves[:, 1], y_tok[:].rearrange("p t d -> p (t d)")]
        scores = [[ctx.enter_context(nc.psum_tensor(f"a_scores{i}{h}", [P, 2, 2 * P], F32)) for h in (0, 1)] for i in (0, 1)]
        bank = [ctx.enter_context(nc.psum_tensor(f"a_bank{i}", [P, 512], F32)) for i in range(3)]
        o_bank = ctx.enter_context(nc.psum_tensor("a_o_bank", [P, CHUNK], F32))

        prepare = {2: "load_x", 4: "norm_stats", 5: "norm_apply", 6: "rms_sum", 7: "rms_scale", 9: "rms_apply",
                   12: "transpose_x", 13: "gates"}
        steps = []
        for s in range(NU + 3):
            k, r = divmod(s, UNITS)
            if s < NU:
                steps.append(("scores", s))
            if s % (2 * UNITS) == 6 and s < NU:
                steps.append(("load_y", s // (2 * UNITS)))
            if r == 6:
                steps.append(("project_qk", PAIRS * (k + 1)))
            elif r in (0, 2) and k >= 1:
                steps.append(("project_qk", PAIRS * k + 1 + r // 2))
            if r == 4 and k >= 1:
                steps.append(("project_out", k - 1))
            if s >= 4 and s % 2 == 0:
                steps.append(("values", (s - 4) // 2))
            if r == 4 and k >= 1:
                steps.append(("project_qk", PAIRS * k + 3))
            if 2 <= s < NU + 2:
                steps.append(("transpose", s - 2))
            if s < NU:
                steps += [("softmax", s), ("weigh", s)]
            if r % 2 == 1 and k < A_GROUPS:
                steps.append(("keep_keys", s // 2))
            if r % 2 == 1 and A_GROUPS - 1 <= k < BLOCKS - 1:
                steps.append(("keys_back", PAIRS * (k + 1) + r // 2))
            if r == 2 and k < BLOCKS:
                steps.append(("project_v", k))
            for h in range(HALVES):
                if s - 2 * UNITS * h in prepare:
                    steps.append((prepare[s - 2 * UNITS * h], h))
        steps += [("project_qk", PAIRS * BLOCKS + 3), ("project_out", BLOCKS - 1)]
        e, a0 = HALVES - 1, PAIRS * BLOCKS
        before = [("load_x", e), ("norm_stats", e), ("norm_apply", e), ("rms_sum", e), ("rms_scale", e), ("split", 0), ("rms_apply", e),
                  ("split", 1), ("transpose_x", e), ("split", 2), ("split", 3), ("split", 4), ("gates", e), ("project_qk", a0), ("split", 5),
                  ("project_qk", a0 + 1), ("split", 6), ("project_qk", a0 + 2), ("split", 7), ("project_qk", a0 + 3), ("split", 8)]

        def count(name, sizes, unit=1, credit=0):
            return Count(nc.alloc_semaphore("a_" + name), before, steps, sizes, unit, credit)

        fills = {"project_qk": 2, "project_v": TILES, "project_out": TILES, "transpose": 2, "transpose_x": CT, "gates": 1}
        highs = {kind: n for kind, n in fills.items() if kind not in ("project_out", "gates")}
        filled = count("filled", fills)
        hi_taken = count("hi_taken", highs)
        emptied = count("emptied", fills)
        scored = count("scored", {"scores": 1})
        maxed = count("maxed", {"scores": 2})
        negated = count("negated", {"scores": 2})
        exped = count("exped", {"scores": 2}, credit=1)
        inverted = count("inverted", {"weigh": 2})
        weighed = count("weighed", {"weigh": 2})
        normalized = count("normalized", {"weigh": 2})
        o_filled = count("o_filled", {"values": 1})
        o_hi_taken = count("o_hi_taken", {"values": 1})
        o_emptied = count("o_emptied", {"values": 1}, credit=1)
        x_loaded = count("x_loaded", {"load_x": 1}, unit=16)
        bn_done = count("bn_done", {"norm_stats": 1})
        aggregated = count("aggregated", {"norm_stats": 1})
        var_ready = count("var_ready", {"norm_stats": 1})
        rstd_ready = count("rstd_ready", {"norm_stats": 1})
        x_normed = count("x_normed", {"norm_apply": 1})
        normed_stored = count("normed_stored", {"norm_apply": 1}, unit=16)
        squared = count("squared", {"rms_sum": TILES})
        ms_ready = count("ms_ready", {"rms_scale": 1})
        rms_ready = count("rms_ready", {"rms_scale": 1})
        x_ready = count("x_ready", {"rms_apply": 1})
        gate_biased = count("gate_biased", {"gates": 1})
        gate_exped = count("gate_exped", {"gates": 1})
        gate_plus_1 = count("gate_plus_1", {"gates": 1})
        gated = count("gated", {"gates": 1})
        keys_kept = count("keys_kept", {"keep_keys": 1}, unit=16, credit=1)
        keys_back = count("keys_back", {"keys_back": 1}, unit=16, credit=1)
        y_loaded = count("y_loaded", {"load_y": 1}, unit=16)
        y_stored = count("y_stored", {"load_y": 1}, unit=16, credit=1)
        consts_loaded = nc.alloc_semaphore("a_consts_loaded")
        staged = [nc.alloc_semaphore(f"a_staged{i}") for i in range(3)]
        stage_hi_taken = nc.alloc_semaphore("a_stage_hi_taken")
        stage_emptied = nc.alloc_semaphore("a_stage_emptied")
        dve_carried, sp_carried = nc.alloc_semaphore("a_dve_carried"), nc.alloc_semaphore("a_sp_carried")
        zero_rows_ready = nc.alloc_semaphore("a_zero_rows_ready")
        zero_rows_stored = nc.alloc_semaphore("a_zero_rows_stored")
        exponent_ready = nc.alloc_semaphore("a_exponent_ready")
        zeroed = nc.alloc_semaphore("a_zeroed")
        CONSTS = 4

        pieces = []
        pieces.append((w_gates.rearrange("(c p) n -> p c n", p=P), wgate[:, HI], wgate[:, LO]))
        for n in range(3):
            for c in range(CT):
                cols = slice(n * A_INNER, (n + 1) * A_INNER)
                pieces.append((w_qkv[c * P:(c + 1) * P, cols], wqkv[:, HI, c, cols], wqkv[:, LO, c, cols]))
        wo_rows = w_out.rearrange("(c p) n -> p c n", p=P)
        for c in range(0, A_INNER // P, 4):
            pieces.append((wo_rows[:, c:c + 4, :], wout[:, HI, c:c + 4, :], wout[:, LO, c:c + 4, :]))

        def stage_of(i):
            shape = pieces[i][1].shape
            if len(shape) == 2:
                return stages[i % 3][:, 0:shape[1]]
            return stages[i % 3][:, 0:shape[1] * shape[2]].rearrange("p (c n) -> p c n", n=shape[2])

        def prepared(it, h):
            return 0 if it is None else (it + (h + 1) // HALVES) % BATCH, (h + 1) % HALVES

        def half_group(k):
            return (k // A_GROUPS) % HALVES, k % A_GROUPS

        def unit_place(u):
            return u // UNITS, u % UNITS // 2, 2 * (u % 2)

        def values_of(half, group, tile):
            return v_kept[:, group] if tile < 0 or (half == 0 and tile == TILES - 1) else v[:, tile]

        def value_operand(half, group, tile, part, pair, head):
            return values_of(half, group, tile)[:, part, pair, head:head + 2, :].rearrange("p b d -> p (b d)")

        def like(source, place):
            if len(place.shape) == 2:
                return source[:]
            return source[:].rearrange("p (a b d) -> p a b d", a=place.shape[1], b=place.shape[2])

        block = ctx.enter_context(nc.Block())

        @block.sync
        def _(sp):
            sp.dma_start(ident[:], identity).then_inc(consts_loaded, 16)
            sp.dma_start(mask[:], masks.rearrange("s p k -> p s k")[:, :, K0:2 * P]).then_inc(consts_loaded, 16)
            sp.dma_start(gamma_row[:], gamma.unsqueeze(0).broadcast_to([P, D])).then_inc(consts_loaded, 16)
            sp.dma_start(bgate_row[:], b_gates.unsqueeze(0).broadcast_to([P, A_HEADS])).then_inc(consts_loaded, 16)
            for each in (y_stored, keys_kept, keys_back):
                sp.sem_inc(each.sem, 1)

            def load_x(it, h):
                if it is not None:
                    sp.wait_ge(filled.sem, filled.past(it, ("transpose_x", h - 1), CT - 1) if h else filled.upto(it, -1))
                sequence, half = prepared(it, h)
                sp.dma_start(x_tok[:], tokens_of(x, sequence, half)).then_inc(x_loaded.sem, 16)

            def store_normed(it, h):
                sp.wait_ge(x_normed.sem, x_normed.past(it, ("norm_apply", h)))
                sequence, half = prepared(it, h)
                sp.dma_start(tokens_of(normed, sequence, half, ahead=1), x_tok[:]).then_inc(normed_stored.sem, 16)

            load_x(None, HALVES - 1)
            for i, (src, _, _) in enumerate(pieces):
                if i == 3:
                    store_normed(None, HALVES - 1)
                if i >= 3:
                    sp.wait_ge(stage_emptied, i - 2)
                sp.dma_start(stage_of(i), src).then_inc(staged[i % 3], 16)
            sp.wait_ge(zero_rows_ready, 1)
            for state in (normed, hidden):
                sp.dma_start(state[:, 0, :], zero_rows[:]).then_inc(zero_rows_stored, 16)
            sp.wait_ge(stage_emptied, len(pieces))
            with sp.Fori(0, BATCH) as it:
                for step in steps:
                    kind, a = step
                    if kind == "load_x":
                        load_x(it, a)
                    elif kind == "norm_apply":
                        store_normed(it, a)
                    elif kind == "load_y":
                        sp.wait_ge(y_stored.sem, y_stored.upto(it, a - 1))
                        sp.sem_inc(sp_carried, 1)
                        sp.dma_start(y_tok[:], tokens_of(x, it, a)).then_inc(y_loaded.sem, 16)
                    elif kind == "keep_keys":
                        sp.wait_ge(emptied.sem, emptied.past(it, ("project_qk", a), 1) if a >= PAIRS else emptied.upto(it, -1))
                        sp.sem_inc(sp_carried, 1)
                        sp.wait_ge(keys_kept.sem, keys_kept.upto(it, keys_kept.number(it, step) - 1))
                        sp.dma_start(k_kept[:, a // PAIRS, :, a % PAIRS, :].bitcast(F32),
                                     kT[:, :, a % PAIRS, CHUNK:CHUNK + A_WINDOW].bitcast(F32)).then_inc(keys_kept.sem, 16)
                    elif kind == "keys_back":
                        k, pair = divmod(a, PAIRS)
                        sp.wait_ge(scored.sem, scored.past(it, ("scores", UNITS * (k - 1) + 2 * pair + 1)))
                        sp.wait_ge(keys_back.sem, keys_back.upto(it, keys_back.number(it, step) - 1))
                        sp.dma_start(kT[:, :, pair, 0:A_WINDOW].bitcast(F32), k_kept[:, k % A_GROUPS, :, pair, :].bitcast(F32)).then_inc(keys_back.sem, 16)
                    elif kind == "project_out" and a % A_GROUPS == A_GROUPS - 1:
                        sp.wait_ge(emptied.sem, emptied.past(it, step, TILES - 1))
                        sp.dma_start(tokens_of(attended, it, a // A_GROUPS), y_tok[:]).then_inc(y_stored.sem, 16)
            sp.wait_ge(y_stored.sem, y_stored.upto(BATCH, -1))
            sp.wait_ge(normed_stored.sem, normed_stored.upto(BATCH, -1))
            sp.wait_ge(zero_rows_stored, 16 * 2)

        @block.gpsimd
        def _(pool):
            pool.memset(zero_rows[:], 0.0).then_inc(zero_rows_ready, 1)
            pool.memset(minus_half[:], -0.5).then_inc(exponent_ready, 1)
            pool.memset(kT[:, :, :, 0:A_WINDOW].bitcast(F32), 0.0)
            for t in range(TILES):
                for part in (HI, LO):
                    pool.memset(v[:, t, part, :, ZERO, :].bitcast(F32), 0.0)
            for group in range(A_GROUPS):
                for part in (HI, LO):
                    pool.memset(v_kept[:, group, part, :, ZERO, :].bitcast(F32), 0.0)

            def power(it, h):
                pool.wait_ge(var_ready.sem, var_ready.past(it, ("norm_stats", h)))
                nc.gpsimd.tensor_tensor(rstd[:], rstd[:], minus_half[:], ALU.pow).then_inc(rstd_ready.sem, 1)

            def rms_power(it, h):
                pool.wait_ge(ms_ready.sem, ms_ready.past(it, ("rms_scale", h)))
                nc.gpsimd.tensor_tensor(rms[:], rms[:], minus_half[:], ALU.pow).then_inc(rms_ready.sem, 1)

            pool.wait_ge(exponent_ready, 1)
            power(None, HALVES - 1)
            rms_power(None, HALVES - 1)
            pool.wait_ge(stage_emptied, len(pieces))
            pool.memset(prob[:, :, :, :, 0:K0], 0.0).then_inc(zeroed, 1)
            pool.wait_ge(zeroed, 1)
            with pool.Fori(0, BATCH) as it:
                for kind, a in steps:
                    if kind == "norm_stats":
                        power(it, a)
                    elif kind == "rms_scale":
                        rms_power(it, a)
                    elif kind == "weigh":
                        for head in (0, 1):
                            pool.wait_ge(weighed.sem, weighed.past(it, (kind, a), head))
                            part = prob[:, a % 2, head, :, K0:2 * P]
                            nc.gpsimd.tensor_tensor(part, part, weight[:, a % 2, head].unsqueeze(2).broadcast_to([P, 2, KEYS]),
                                                    ALU.mult).then_inc(normalized.sem, 1)

        @block.tensor
        def _(pe):
            def take_bank(it, n):
                if n >= 3 or it is not None:
                    pe.wait_ge(emptied.sem, emptied.upto(it, n - 3 if n >= 3 else -1))
                return bank[n % 3]

            def products(out, lhs, rhs, tiles):
                order = [(c, a, b) for c in range(tiles) for a, b in PASSES]
                for i, (c, a, b) in enumerate(order):
                    last = nc.tensor.matmul(out, lhs(c, a), rhs(c, b), start=(i == 0), stop=(i == len(order) - 1))
                return last

            def transpose_x(it, h):
                pe.wait_ge(x_ready.sem, x_ready.past(it, ("rms_apply", h)))
                for c in range(CT):
                    out = take_bank(it, filled.number(it, ("transpose_x", h), c))
                    for t in range(TILES):
                        last = nc.tensor.transpose(out[:, t * P:(t + 1) * P], x_tok[:, t, c * P:(c + 1) * P], ident[:])
                    last.then_inc(filled.sem, 1)

            def gates(it, h):
                pe.wait_ge(emptied.sem, emptied.past(it, ("transpose_x", h), CT - 1))
                out = take_bank(it, filled.number(it, ("gates", h)))
                for t in range(TILES):
                    last = products(out[:, t * A_HEADS:(t + 1) * A_HEADS], lambda c, part: xT[:, part, c, t * P:(t + 1) * P],
                                    lambda c, part: wgate[:, part, c, :], CT)
                last.then_inc(filled.sem, 1)

            def project_qk(it, a):
                k, pair = divmod(a, PAIRS)
                _, group = half_group(k)
                if k % A_GROUPS == 0 and pair == 0:
                    pe.wait_ge(emptied.sem, emptied.past(it, ("transpose_x", k // A_GROUPS - 1), CT - 1))
                for which in (0, 1):
                    out = take_bank(it, filled.number(it, ("project_qk", a), which))
                    col = which * A_INNER + (group * PAIRS + pair) * P
                    products(out[:], lambda c, part: wqkv[:, part, c, col:col + P], lambda c, part: xT[:, part, c, :],
                             CT).then_inc(filled.sem, 1)

            pe.wait_ge(consts_loaded, 16 * CONSTS)
            transpose_x(None, HALVES - 1)
            pe.wait_ge(stage_emptied, 5)
            gates(None, HALVES - 1)
            for pair in range(PAIRS):
                project_qk(None, PAIRS * BLOCKS + pair)
            pe.wait_ge(stage_emptied, len(pieces))
            pe.wait_ge(zeroed, 1)
            with pe.Fori(0, BATCH) as it:
                for kind, a in steps:
                    if kind == "project_qk":
                        project_qk(it, a)
                    elif kind == "scores":
                        k, pair, tile = unit_place(a)
                        half, group = half_group(k)
                        if tile == 0:
                            pe.wait_ge(emptied.sem, emptied.past(it, ("project_qk", PAIRS * k + pair), 1) if k else emptied.upto(it, -1))
                            if half:
                                pe.wait_ge(keys_back.sem, keys_back.past(it, ("keys_back", PAIRS * k + pair)))
                        pe.wait_ge(exped.sem, exped.past(it, ("scores", a - 2), 1) if a >= 2 else exped.upto(it, -1))
                        for t in (0, 1):
                            col = (tile + t) * P
                            for i, (qp, kp) in enumerate(PASSES):
                                for head in (0, 1):
                                    rows = slice(DH * head, DH * (head + 1))
                                    mm = nc.tensor.matmul(scores[a % 2][head][:, t, K0:2 * P], q_o[rows, group, qp, pair, col:col + P],
                                                          kT[rows, kp, pair, col:col + KEYS], start=(i == 0), stop=(i == 2))
                        mm.then_inc(scored.sem, 1)
                    elif kind == "transpose":
                        for head in (0, 1):
                            out = take_bank(it, filled.number(it, (kind, a), head))
                            pe.wait_ge(normalized.sem, normalized.past(it, ("weigh", a), head))
                            for j in range(4):
                                last = nc.tensor.transpose(out[:, j * P:(j + 1) * P], prob[:, a % 2, head, j // 2, (j % 2) * P:(j % 2 + 1) * P],
                                                           ident[:])
                            last.then_inc(filled.sem, 1)
                    elif kind == "values":
                        k, pair = divmod(a, PAIRS)
                        half, group = half_group(k)
                        pe.wait_ge(emptied.sem, emptied.past(it, ("transpose", 2 * a + 1), 1))
                        pe.wait_ge(o_emptied.sem, o_emptied.upto(it, a - 1))
                        order = [(kt, head, vp, pp) for kt in key_tiles(half) for head in (0, 1) for vp, pp in PASSES]
                        for i, ((tile, p0, p1, o0, o1), head, vp, pp) in enumerate(order):
                            mm = nc.tensor.matmul(o_bank[:, o0:o1], value_operand(half, group, tile, vp, pair, head),
                                                  probT[:, pp, head, p0:p1], start=(i == 0), stop=(i == len(order) - 1),
                                                  skip_group_check=True)
                        mm.then_inc(o_filled.sem, 1)
                    elif kind == "project_v":
                        _, group = half_group(a)
                        for t in range(TILES):
                            out = take_bank(it, filled.number(it, (kind, a), t))
                            col = 2 * A_INNER + group * GC
                            products(out[:], lambda c, part: xT[:, part, c, t * P:(t + 1) * P], lambda c, part: wqkv[:, part, c, col:col + GC],
                                     CT).then_inc(filled.sem, 1)
                    elif kind == "project_out":
                        _, group = half_group(a)
                        pe.wait_ge(o_emptied.sem, o_emptied.past(it, ("values", PAIRS * (a + 1) - 1)))
                        for t in range(TILES):
                            out = take_bank(it, filled.number(it, (kind, a), t))
                            products(out[:, 0:D], lambda c, part: q_o[:, group, part, c, t * P:(t + 1) * P],
                                     lambda c, part: wout[:, part, group * PAIRS + c, :], PAIRS).then_inc(filled.sem, 1)
                    elif kind == "transpose_x":
                        transpose_x(it, a)
                    elif kind == "gates":
                        gates(it, a)

        def high_targets(it, kind, a):
            if kind == "project_qk":
                k, pair = divmod(a, PAIRS)
                _, group = half_group(k)
                return [lambda part: q_o[:, group, part, pair, :], lambda part: kT[:, part, pair, A_WINDOW:A_WINDOW + CHUNK]]
            if kind == "project_v":
                half, group = half_group(a)
                return [(lambda part, t=t: values_of(half, group, t)[:, part, :, VALUE:VALUE_2 + 1:2, :]) for t in range(TILES)]
            if kind == "transpose":
                return [(lambda part, head=head: probT[:, part, head, a % 2 * 4 * P:(a % 2 + 1) * 4 * P]) for head in (0, 1)]
            assert kind == "transpose_x"
            return [(lambda part, c=c: xT[:, part, c, :]) for c in range(CT)]

        @block.scalar
        def _(act):
            act.sem_inc(exped.sem, 1)
            def take_high(it, kind, a):
                for i, place in enumerate(high_targets(it, kind, a)):
                    n = filled.number(it, (kind, a), i)
                    act.wait_ge(filled.sem, filled.upto(it, n))
                    nc.scalar.activation(place(HI), like(bank[n % 3], place(HI)), ACT.Copy).then_inc(hi_taken.sem, 1)

            def rms_sum(it, h):
                act.wait_ge(x_normed.sem, x_normed.past(it, ("norm_apply", h)))
                for t in range(TILES):
                    if it is not None or t:
                        act.wait_ge(squared.sem, squared.upto(it, squared.number(it, ("rms_sum", h), t) - 1))
                    nc.scalar.activation(square[:], x_tok[:, t, :], ACT.Square, accum_out=sumsq[:, t:t + 1]).then_inc(squared.sem, 1)

            def gates(it, h):
                act.wait_ge(gate_biased.sem, gate_biased.past(it, ("gates", h)))
                nc.scalar.activation(gate_in[:], gate_in[:], ACT.Exp, scale=-1.0).then_inc(gate_exped.sem, 1)

            for kind, a in before:
                if kind == "split":
                    act.wait_ge(staged[a % 3], 16 * (a // 3 + 1))
                    nc.scalar.activation(pieces[a][1], stage_of(a), ACT.Copy).then_inc(stage_hi_taken, 1)
                elif kind == "rms_sum":
                    rms_sum(None, a)
                elif kind == "gates":
                    gates(None, a)
                elif kind in highs:
                    take_high(None, kind, a)
            with act.Fori(0, BATCH) as it:
                for kind, a in steps:
                    if kind == "project_qk" and PAIRS <= a < PAIRS * (A_GROUPS + 1):
                        act.wait_ge(keys_kept.sem, keys_kept.past(it, ("keep_keys", a - PAIRS)))
                    if kind in highs:
                        take_high(it, kind, a)
                    elif kind == "softmax":
                        for head in (0, 1):
                            act.wait_ge(negated.sem, negated.past(it, ("scores", a), head))
                            for t in (0, 1):
                                e = nc.scalar.activation(prob[:, a % 2, head, t, K0:2 * P], scores[a % 2][head][:, t, K0:2 * P], ACT.Exp,
                                                         bias=neg_max[:, a % 2, head, t:t + 1], scale=DH ** -0.5,
                                                         accum_out=row_sum[:, a % 2, head, t:t + 1])
                            e.then_inc(exped.sem, 1)
                    elif kind == "values":
                        _, group = half_group(a // PAIRS)
                        act.wait_ge(o_filled.sem, o_filled.past(it, (kind, a)))
                        nc.scalar.activation(q_o[:, group, HI, a % PAIRS, :], o_bank[:], ACT.Copy).then_inc(o_hi_taken.sem, 1)
                    elif kind == "rms_sum":
                        rms_sum(it, a)
                    elif kind == "gates":
                        gates(it, a)

        @block.vector
        def _(dve):
            dve.sem_inc(o_emptied.sem, 1)
            def take_low(it, kind, a):
                for i, place in enumerate(high_targets(it, kind, a)):
                    n = filled.number(it, (kind, a), i)
                    dve.wait_ge(hi_taken.sem, hi_taken.past(it, (kind, a), i))
                    nc.vector.tensor_tensor(place(LO), like(bank[n % 3], place(LO)), place(HI).bitcast(F32), ALU.subtract).then_inc(emptied.sem, 1)

            def norm_stats(it, h):
                dve.wait_ge(x_loaded.sem, x_loaded.past(it, ("load_x", h)))
                for t in range(TILES):
                    last = nc.vector.bn_stats(bn[:, t, :], x_tok[:, t, :])
                last.then_inc(bn_done.sem, 1)
                dve.wait_ge(bn_done.sem, bn_done.past(it, ("norm_stats", h)))
                dve.sem_inc(dve_carried, 1)
                for t in range(TILES):
                    last = nc.vector.bn_aggr(mean_var[:, t, :], bn[:, t, :])
                last.then_inc(aggregated.sem, 1)
                dve.wait_ge(aggregated.sem, aggregated.past(it, ("norm_stats", h)))
                nc.vector.tensor_scalar(rstd[:], mean_var[:, :, 1], 1e-5, None, ALU.add).then_inc(var_ready.sem, 1)

            def norm_apply(it, h):
                dve.wait_ge(rstd_ready.sem, rstd_ready.past(it, ("norm_stats", h)))
                for t in range(TILES):
                    last = nc.vector.tensor_scalar(x_tok[:, t, :], x_tok[:, t, :], mean_var[:, t, 0:1], rstd[:, t:t + 1], ALU.subtract, ALU.mult)
                last.then_inc(x_normed.sem, 1)

            def rms_scale(it, h):
                dve.wait_ge(squared.sem, squared.past(it, ("rms_sum", h), TILES - 1))
                nc.vector.tensor_scalar(rms[:], sumsq[:], 1e-24, 1.0 / D, ALU.max, ALU.mult).then_inc(ms_ready.sem, 1)

            def rms_apply(it, h):
                dve.wait_ge(rms_ready.sem, rms_ready.past(it, ("rms_scale", h)))
                dve.wait_ge(normed_stored.sem, normed_stored.past(it, ("norm_apply", h)))
                for t in range(TILES):
                    last = nc.vector.scalar_tensor_tensor(out=x_tok[:, t, :], in0=x_tok[:, t, :], scalar=rms[:, t:t + 1], in1=gamma_row[:],
                                                          op0=ALU.mult, op1=ALU.mult)
                last.then_inc(x_ready.sem, 1)

            def gates(it, h):
                n = filled.number(it, ("gates", h))
                dve.wait_ge(filled.sem, filled.upto(it, n))
                logits = bank[n % 3][:, 0:TILES * A_HEADS].rearrange("p (t h) -> p t h", t=TILES)
                g = nc.vector.tensor_tensor(gate_in[:], logits, bgate_row[:].unsqueeze(1).broadcast_to([P, TILES, A_HEADS]), ALU.add)
                g.then_inc(gate_biased.sem, 1)
                dve.wait_ge(gate_exped.sem, gate_exped.past(it, ("gates", h)))
                nc.vector.tensor_scalar(gate_in[:], gate_in[:], 1.0, None, ALU.add).then_inc(gate_plus_1.sem, 1)
                dve.wait_ge(gate_plus_1.sem, gate_plus_1.past(it, ("gates", h)))
                nc.vector.reciprocal(gate[:, (h + 1) % HALVES], gate_in[:]).then_inc(gated.sem, 1)
                dve.sem_inc(emptied.sem, 1)

            prepare_steps = {"norm_stats": norm_stats, "norm_apply": norm_apply, "rms_scale": rms_scale, "rms_apply": rms_apply, "gates": gates}
            for kind, a in before:
                if kind == "split":
                    _, hi, lo = pieces[a]
                    dve.wait_ge(stage_hi_taken, a + 1)
                    nc.vector.tensor_tensor(lo, stage_of(a), hi.bitcast(F32), ALU.subtract).then_inc(stage_emptied, 1)
                elif kind == "rms_apply":
                    dve.wait_ge(consts_loaded, 16 * CONSTS)
                    rms_apply(None, a)
                elif kind in prepare_steps:
                    prepare_steps[kind](None, a)
                elif kind in highs:
                    take_low(None, kind, a)
            with dve.Fori(0, BATCH) as it:
                for kind, a in steps:
                    if kind == "scores":
                        k, _, tile = unit_place(a)
                        half, _ = half_group(k)
                        dve.wait_ge(scored.sem, scored.past(it, (kind, a)))
                        dve.sem_inc(dve_carried, 1)
                        for head in (0, 1):
                            for t in (0, 1):
                                s = scores[a % 2][head][:, t, K0:2 * P]
                                m = nc.vector.tensor_tensor_reduce(out=s, in0=s, in1=mask[:, min(half * TILES + tile + t, 1)], scale=1.0, scalar=-3e38,
                                                                   op0=ALU.add, op1=ALU.max, accum_out=row_max[:, a % 2, head, t:t + 1])
                            m.then_inc(maxed.sem, 1)
                            dve.wait_ge(maxed.sem, maxed.past(it, (kind, a), head))
                            nc.vector.tensor_scalar(neg_max[:, a % 2, head], row_max[:, a % 2, head], -DH ** -0.5, None,
                                                    ALU.mult).then_inc(negated.sem, 1)
                    elif kind in highs:
                        take_low(it, kind, a)
                    elif kind == "weigh":
                        k, pair, tile = unit_place(a)
                        half, group = half_group(k)
                        if a % (2 * UNITS) == 0:
                            dve.wait_ge(gated.sem, gated.upto(it, half - 1))
                        for head in (0, 1):
                            dve.wait_ge(exped.sem, exped.past(it, ("scores", a), head))
                            nc.vector.reciprocal(row_inv[:, a % 2, head], row_sum[:, a % 2, head]).then_inc(inverted.sem, 1)
                            dve.wait_ge(inverted.sem, inverted.past(it, (kind, a), head))
                            nc.vector.tensor_tensor(weight[:, a % 2, head], row_inv[:, a % 2, head],
                                                    gate[:, half, tile:tile + 2, group * GROUP + 2 * pair + head], ALU.mult).then_inc(weighed.sem, 1)
                    elif kind == "values":
                        _, group = half_group(a // PAIRS)
                        dve.wait_ge(o_hi_taken.sem, o_hi_taken.past(it, (kind, a)))
                        nc.vector.tensor_tensor(q_o[:, group, LO, a % PAIRS, :], o_bank[:], q_o[:, group, HI, a % PAIRS, :].bitcast(F32),
                                                ALU.subtract).then_inc(o_emptied.sem, 1)
                    elif kind == "project_out":
                        half, group = half_group(a)
                        if group == 0:
                            dve.wait_ge(y_loaded.sem, y_loaded.past(it, ("load_y", half)))
                        for t in range(TILES):
                            n = filled.number(it, (kind, a), t)
                            dve.wait_ge(filled.sem, filled.upto(it, n))
                            nc.vector.tensor_tensor(y_tok[:, t, :], bank[n % 3][:, 0:D], y_tok[:, t, :], ALU.add).then_inc(emptied.sem, 1)
                    elif kind == "norm_stats":
                        norm_stats(it, a)
                    elif kind == "norm_apply":
                        norm_apply(it, a)
                    elif kind == "rms_scale":
                        rms_scale(it, a)
                    elif kind == "rms_apply":
                        rms_apply(it, a)
                    elif kind == "gates":
                        gates(it, a)


F_HEADS, F_WINDOW, F_DEPTH = 8, 128, 2
F_INNER = F_HEADS * DH
HID = D * 4 * 2 // 3
FH = 6
HT = -(-HID // FH)
HL = HID - (FH - 1) * HT
QUERY, KEY = 0, 1
COS, SIN = 0, 1


def ffn_phase(nc, layer, state_in, state_out, ahead_out, attended, wqkv_in, q_scale, k_scale, wo_in, ln_g, ln_b, w1_in, b1, w2_in, b2,
              masks, identity, tables_in):
    with ExitStack() as ctx:
        def sb(name, shape, dt=F32):
            return ctx.enter_context(nc.sbuf_tensor(f"f{layer}_{name}", shape, dt))

        NU = HALVES * UNITS

        wqkv = sb("wqkv", [P, 2, CT, 3 * F_INNER], F32R)
        wo = sb("wo", [P, 2, PAIRS, D], F32R)
        w1 = sb("w1", [P, 2, CT, 2 * HID], F32R)
        w2 = sb("w2", [P, 2, FH, D], F32R)
        b1_cols = sb("b1_cols", [P, 2, FH])
        ln_g_row = sb("ln_g_row", [P, D])
        ln_b_row = sb("ln_b_row", [P, D])
        b2_row = sb("b2_row", [P, D])
        scale_rows = sb("scale_rows", [P, 2, 2, DH])
        ident = sb("ident", [P, P])
        mask = sb("mask", [P, 2, 2 * P])
        edge = sb("edge", [1, HALVES, P])
        minus_half = sb("minus_half", [P, 2 * F_HEADS])
        x_tok = sb("x_tok", [P, TILES, D])
        x1 = sb("x1", [P, TILES, D])
        actT = sb("actT", [P, 2, CT, CHUNK], F32R)
        q_o = sb("q_o", [P, 2, PAIRS, CHUNK], F32R)
        kT = sb("kT", [P, 2, PAIRS, P + CHUNK], F32R)
        v = sb("v", [P, TILES, 2, PAIRS, 3, DH], F32R)
        v_kept = sb("v_kept", [P, 2, PAIRS, 3, DH], F32R)
        probT = sb("probT", [P, 2, 2, 2 * TILES * P], F32R)
        prob = sb("prob", [P, 2, 2, 2, 2 * P])
        tables = sb("tables", [P, 2, 2, TILES, DH])
        qk_tok = sb("qk_tok", [P, TILES, 2, F_INNER])
        sin_part = sb("sin_part", [P, 2, F_INNER])
        gu = sb("gu", [P, 2, CHUNK])
        square = gu
        norm = sb("norm", [P, TILES, 2, F_HEADS])
        bn = sb("bn", [P, TILES, 2, 6])
        mean_var = sb("mean_var", [P, TILES, 2])
        rstd = sb("rstd", [P, TILES])
        row_max = sb("row_max", [P, 2, 2, 2])
        neg_max = sb("neg_max", [P, 2, 2, 2])
        row_sum = sb("row_sum", [P, 2, 2, 2])
        weight = sb("weight", [P, 2, 2, 2])
        halves = prob[:].rearrange("p a b c d -> p (a b c d)").rearrange("p (s n) -> p s n", s=2)
        stages = [halves[:, 0], halves[:, 1], x1[:].rearrange("p t d -> p (t d)")]
        u = probT[:].rearrange("p a b c -> p (a b c)").rearrange("p (s a n) -> p s a n", s=4, a=2)
        scores = [[ctx.enter_context(nc.psum_tensor(f"f{layer}_scores{i}{h}", [P, 2, 2 * P], F32)) for h in (0, 1)] for i in (0, 1)]
        bank = [ctx.enter_context(nc.psum_tensor(f"f{layer}_bank{i}", [P, 512], F32)) for i in range(3)]
        o_bank = ctx.enter_context(nc.psum_tensor(f"f{layer}_o_bank", [P, CHUNK], F32))
        y_banks = scores[1]

        steps = []
        for h in range(HALVES):
            u0, p0, t0, j0 = h * UNITS, h * PAIRS, h * TILES, h * FH
            early = {0: [("load_x", h), ("load_tables", h)], 1: [("scale_tables", h)], 2: [("transpose_x", h)], 4: [("load_x1", h)],
                     5: [("rope", t0)], 7: [("rope_sum", t0), ("rope", t0 + 1)]}
            for s in range(UNITS):
                n = u0 + s
                steps.append(("scores", n))
                if s in (4, 6):
                    steps += [("project_qk", t0 + (s - 4) // 2), ("values", p0 + (s - 4) // 2)]
                if s >= 2:
                    steps.append(("transpose", n - 2))
                steps += [("softmax", n), ("weigh", n)] + early.get(s, [])
            if h == 0:
                steps.append(("shift_keys", h))
            steps += [("project_qk", t0 + 2), ("values", p0 + 2), ("transpose", u0 + 6),
                      ("transpose", u0 + 7), ("rope_sum", t0 + 1), ("rope", t0 + 2), ("project_qk", t0 + 3), ("values", p0 + 3), ("project_o", h), ("shift_front", h),
                      ("shift_back", h), ("ln_stats", 2 * h), ("project_v", h), ("ln_apply", 2 * h), ("ln_stats", 2 * h + 1),
                      ("transpose_qk", t0), ("ln_apply", 2 * h + 1), ("transpose_qk", t0 + 1), ("transpose_h", h), ("x1_bias", h),
                      ("rope_sum", t0 + 2), ("rope", t0 + 3), ("up", j0)]
            between = {1: ("transpose_qk", t0 + 2), 2: ("rope_sum", t0 + 3), FH - 1: ("transpose_qk", t0 + 3)}
            for j in range(1, FH):
                steps.append(("up", j0 + j))
                if j in between:
                    steps.append(between[j])
                steps.append(("down", j0 + j - 1))
                if j == 3 and attended is not None:
                    steps.append(("add_attended", h))
            steps += [("down", j0 + FH - 1), ("out", h)]
        e, t0 = HALVES - 1, (HALVES - 1) * TILES
        before = [("load_x", e), ("load_tables", e), ("split", 0), ("transpose_x", e), ("split", 1), ("split", 2), ("split", 3),
                  ("scale_tables", e), ("project_qk", t0), ("project_qk", t0 + 1), ("rope", t0), ("split", 4), ("project_qk", t0 + 2),
                  ("rope_sum", t0), ("rope", t0 + 1), ("split", 5), ("project_qk", t0 + 3), ("rope_sum", t0 + 1), ("rope", t0 + 2),
                  ("split", 6), ("transpose_qk", t0), ("project_v", e), ("rope_sum", t0 + 2), ("rope", t0 + 3), ("split", 7),
                  ("transpose_qk", t0 + 1), ("rope_sum", t0 + 3), ("split", 8), ("transpose_qk", t0 + 2), ("split", 9),
                  ("transpose_qk", t0 + 3), ("split", 10), ("split", 11)]

        def sem(name):
            return nc.alloc_semaphore(f"f{layer}_{name}")

        def count(name, sizes, unit=1, credit=0):
            return Count(sem(name), before, steps, sizes, unit, credit)

        fills = {"project_qk": 2, "project_v": TILES, "project_o": TILES, "transpose": 2, "transpose_x": CT, "transpose_h": CT,
                 "transpose_qk": 2, "up": 2}
        highs = {kind: n for kind, n in fills.items() if kind not in ("project_qk", "project_o", "up")}
        filled = count("filled", fills)
        hi_taken = count("hi_taken", highs)
        emptied = count("emptied", fills)
        scored = count("scored", {"scores": 1})
        maxed = count("maxed", {"scores": 2})
        negated = count("negated", {"scores": 2})
        exped = count("exped", {"scores": 2}, credit=1)
        weighed = count("weighed", {"weigh": 2})
        normalized = count("normalized", {"weigh": 2})
        o_filled = count("o_filled", {"values": 1})
        o_hi_taken = count("o_hi_taken", {"values": 1})
        o_emptied = count("o_emptied", {"values": 1}, credit=1)
        x_loaded = count("x_loaded", {"load_x": 1}, unit=32)
        tables_loaded = count("tables_loaded", {"load_tables": 1}, unit=16)
        tables_ready = count("tables_ready", {"scale_tables": 1})
        x1_loaded = count("x1_loaded", {"load_x1": 1}, unit=16)
        keys_shifted = count("keys_shifted", {"shift_keys": 1}, unit=16)
        raw_taken = count("raw_taken", {"project_qk": 2})
        clamped = count("clamped", {"project_qk": 1})
        norm_ready = count("norm_ready", {"project_qk": 1})
        sin_ready = count("sin_ready", {"rope": 1})
        cos_ready = count("cos_ready", {"rope": 1})
        rope_added = count("rope_added", {"rope_sum": 1})
        roped = count("roped", {"rope_sum": 1})
        shifted = [count("front_shifted", {"shift_front": 1}, unit=48), count("back_shifted", {"shift_back": 1}, unit=32)]
        edge_kept = count("edge_kept", {"shift_keys": 1}, unit=16)
        bn_done = count("bn_done", {"ln_stats": 1})
        aggregated = count("aggregated", {"ln_stats": 1})
        var_ready = count("var_ready", {"ln_stats": 1})
        rstd_ready = count("rstd_ready", {"ln_stats": 1})
        ln_scaled = count("ln_scaled", {"ln_apply": 1})
        ln_ready = count("ln_ready", {"ln_apply": 1})
        x1_biased = count("x1_biased", {"x1_bias": 1})
        attended_loaded = count("attended_loaded", {"add_attended": 1}, unit=16)
        attended_added = count("attended_added", {"add_attended": 1}, credit=1)
        gelued = count("gelued", {"up": 1})
        u_hi = count("u_hi", {"up": 1})
        u_ready = count("u_ready", {"up": 1})
        downed = count("downed", {"down": 1})
        x2_ready = count("x2_ready", {"out": 2}, credit=1)
        x2_stored = count("x2_stored", {"out": 1}, unit=16, credit=1)
        ident_loaded = sem("ident_loaded")
        scales_loaded = sem("scales_loaded")
        consts_loaded = sem("consts_loaded")
        staged = [sem(f"staged{i}") for i in range(3)]
        stage_hi_taken = sem("stage_hi_taken")
        stage_emptied = sem("stage_emptied")
        dve_carried, sp_carried = sem("dve_carried"), sem("sp_carried")
        zeroed = sem("zeroed")

        pieces = []
        for c in range(CT):
            rows = slice(c * P, (c + 1) * P)
            for c0, c1 in ((0, 2 * F_INNER), (2 * F_INNER, 3 * F_INNER)):
                pieces.append((wqkv_in[rows, c0:c1], wqkv[:, HI, c, c0:c1], wqkv[:, LO, c, c0:c1]))
        pieces.append((wo_in.rearrange("(c p) n -> p c n", p=P), wo[:, HI], wo[:, LO]))
        for c in range(CT):
            rows = slice(c * P, (c + 1) * P)
            for c0, c1 in ((0, HID), (HID, 2 * HID)):
                pieces.append((w1_in[rows, c0:c1], w1[:, HI, c, c0:c1], w1[:, LO, c, c0:c1]))
        for j0, j1, m in ((0, 4, HT), (4, FH - 1, HT), (FH - 1, FH, HL)):
            r0 = j0 * HT
            pieces.append((w2_in[r0:r0 + (j1 - j0) * m, :].rearrange("(j p) n -> p j n", p=m), w2[0:m, HI, j0:j1, :], w2[0:m, LO, j0:j1, :]))

        def stage_of(i):
            shape = pieces[i][1].shape
            if len(shape) == 2:
                return stages[i % 3][:, 0:shape[1]]
            return stages[i % 3][0:shape[0], 0:shape[1] * shape[2]].rearrange("p (c n) -> p c n", n=shape[2])

        def prepared(it, h):
            return 0 if it is None else (it + (h + 1) // HALVES) % BATCH, (h + 1) % HALVES

        def values_of(half, tile):
            return v_kept[:] if tile < 0 or (half == 0 and tile == TILES - 1) else v[:, tile]

        def value_operand(half, tile, part, pair, head):
            return values_of(half, tile)[:, part, pair, head:head + 2, :].rearrange("p b d -> p (b d)")

        def like(source, place):
            if len(place.shape) == 2:
                return source[:]
            if len(place.shape) == 3:
                return source[:].rearrange("p (a d) -> p a d", a=place.shape[1])
            return source[:].rearrange("p (a b d) -> p a b d", a=place.shape[1], b=place.shape[2])

        def by_head(a):
            return a.rearrange("p i (h d) -> p i h d", d=DH)

        def table(kind, tile):
            return tables[:, :, kind, tile, :].unsqueeze(2).broadcast_to([P, 2, F_HEADS, DH])

        def hidden_of(a):
            j = a % FH
            return j, HL if j == FH - 1 else HT

        def places_of(kind, a):
            if kind == "project_v":
                half = (a + 1) % HALVES
                return [(lambda part, t=t: values_of(half, t)[:, part, :, VALUE:VALUE_2 + 1:2, :]) for t in range(TILES)]
            if kind == "transpose":
                return [(lambda part, head=head: probT[:, part, head, a % 2 * 4 * P:(a % 2 + 1) * 4 * P]) for head in (0, 1)]
            if kind == "transpose_qk":
                col = a % TILES * P
                return [lambda part: q_o[:, part, :, col:col + P], lambda part: kT[:, part, :, P + col:2 * P + col]]
            assert kind in ("transpose_x", "transpose_h")
            return [(lambda part, c=c: actT[:, part, c, :]) for c in range(CT)]

        CONSTS, SCALES = 8, 6
        block = ctx.enter_context(nc.Block())

        @block.sync
        def _(sp):
            sp.sem_inc(x2_stored.sem, 1)
            sp.sem_inc(attended_added.sem, 1)

            def load_x(it, h):
                if it is not None:
                    if attended is None or h == 0:
                        sp.wait_ge(filled.sem, filled.past(it, ("transpose_h", h - 1), CT - 1) if h else filled.upto(it, -1))
                    if attended is not None:
                        sp.wait_ge(attended_added.sem, attended_added.upto(it, h - 1))
                sequence, half = prepared(it, h)
                sp.dma_start(x_tok[:, :, 0:P], tokens_of(state_in, sequence, half, ahead=1)[:, :, 0:P]).then_inc(x_loaded.sem, 16)
                sp.dma_start(x_tok[:, :, P:D], tokens_of(state_in, sequence, half, ahead=0)[:, :, P:D]).then_inc(x_loaded.sem, 16)

            def load_tables(it, h):
                if it is not None:
                    sp.wait_ge(roped.sem, roped.upto(it, h * TILES - 1))
                sp.dma_start(tables[:], tables_in[(h + 1) % HALVES]).then_inc(tables_loaded.sem, 16)

            load_x(None, HALVES - 1)
            sp.dma_start(ident[:], identity).then_inc(ident_loaded, 16)
            load_tables(None, HALVES - 1)

            def stage_piece(i):
                if i >= 3:
                    sp.wait_ge(stage_emptied, i - 2)
                sp.dma_start(stage_of(i), pieces[i][0]).then_inc(staged[i % 3], 16)

            for i in range(4):
                stage_piece(i)
            for which, row in ((QUERY, q_scale), (KEY, k_scale)):
                row = row.unsqueeze(0).broadcast_to([P, DH])
                sp.dma_start(scale_rows[:, which, COS, :], row).then_inc(scales_loaded, 16)
                sp.dma_start(scale_rows[:, which, SIN, 0:DH // 2], row[:, DH // 2:DH]).then_inc(scales_loaded, 16)
                sp.dma_start(scale_rows[:, which, SIN, DH // 2:DH], row[:, 0:DH // 2]).then_inc(scales_loaded, 16)
            sp.dma_start(mask[:], masks.rearrange("s p k -> p s k")).then_inc(consts_loaded, 16)
            for row, place in ((ln_g, ln_g_row), (ln_b, ln_b_row), (b2, b2_row)):
                sp.dma_start(place[:], row.unsqueeze(0).broadcast_to([P, D])).then_inc(consts_loaded, 16)
            for which in (0, 1):
                c0, c1 = which * HID, which * HID + (FH - 1) * HT
                sp.dma_start(b1_cols[0:HT, which, 0:FH - 1], b1[c0:c1].rearrange("(j p) -> p j", p=HT), allow_slow_non_contiguous=True).then_inc(consts_loaded, 16)
                sp.dma_start(b1_cols[0:HL, which, FH - 1:FH], b1[c1:c0 + HID].rearrange("(j p) -> p j", p=HL), allow_slow_non_contiguous=True).then_inc(consts_loaded, 16)
            for i in range(4, len(pieces)):
                stage_piece(i)
            sp.wait_ge(zeroed, 1)
            sp.wait_ge(stage_emptied, len(pieces))
            with sp.Fori(0, BATCH) as it:
                for kind, a in steps:
                    if kind == "load_x":
                        load_x(it, a)
                    elif kind == "load_tables":
                        load_tables(it, a)
                    elif kind == "load_x1":
                        sp.wait_ge(x2_stored.sem, x2_stored.upto(it, a - 1))
                        sp.sem_inc(sp_carried, 1)
                        sp.dma_start(x1[:], tokens_of(state_in, it, a, ahead=1)).then_inc(x1_loaded.sem, 16)
                    elif kind == "shift_keys":
                        sp.wait_ge(scored.sem, scored.past(it, ("scores", (a + 1) * UNITS - 1)))
                        sp.dma_start(kT[:, :, :, 0:P].bitcast(F32), kT[:, :, :, CHUNK:CHUNK + P].bitcast(F32)).then_inc(keys_shifted.sem, 16)
                    elif kind == "shift_front":
                        sp.wait_ge(emptied.sem, emptied.past(it, ("project_o", a), 1))
                        sp.dma_start(x_tok[1:P, 0:2, P:D], x1[0:P - 1, 0:2, P:D]).then_inc(shifted[0].sem, 16)
                        sp.dma_start(x_tok[0:1, 1, P:D], x1[P - 1:P, 0, P:D]).then_inc(shifted[0].sem, 16)
                        if a:
                            sp.wait_ge(edge_kept.sem, edge_kept.past(it, ("shift_keys", 0)))
                        sp.dma_start(x_tok[0:1, 0, P:D], edge[:, a, :]).then_inc(shifted[0].sem, 16)
                    elif kind == "shift_back":
                        sp.wait_ge(emptied.sem, emptied.past(it, ("project_o", a), TILES - 1))
                        sp.dma_start(x_tok[1:P, 2:TILES, P:D], x1[0:P - 1, 2:TILES, P:D]).then_inc(shifted[1].sem, 16)
                        sp.dma_start(x_tok[0:1, 2:TILES, P:D], x1[P - 1:P, 1:TILES - 1, P:D]).then_inc(shifted[1].sem, 16)
                        if a == 0:
                            sp.dma_start(edge[:, 1, :], x1[P - 1:P, TILES - 1, P:D]).then_inc(edge_kept.sem, 16)
                    elif kind == "add_attended":
                        sp.wait_ge(filled.sem, filled.past(it, ("transpose_h", a), CT - 1))
                        sp.dma_start(x_tok[:], tokens_of(attended, it, a)).then_inc(attended_loaded.sem, 16)
                    elif kind == "out":
                        sp.wait_ge(x2_ready.sem, x2_ready.past(it, (kind, a), 1))
                        sp.dma_start(tokens_of(state_out, it, a, ahead=ahead_out), x1[:]).then_inc(x2_stored.sem, 16)
            sp.wait_ge(x2_stored.sem, x2_stored.upto(BATCH, -1))

        @block.gpsimd
        def _(pool):
            pool.memset(minus_half[:], -0.5)
            pool.memset(edge[:], 0.0)
            pool.memset(kT[:, :, :, 0:P].bitcast(F32), 0.0)
            for t in range(TILES):
                for part in (HI, LO):
                    pool.memset(v[:, t, part, :, ZERO, :].bitcast(F32), 0.0)
            for part in (HI, LO):
                last = pool.memset(v_kept[:, part, :, ZERO, :].bitcast(F32), 0.0)
            last.then_inc(zeroed, 1)
            pool.wait_ge(zeroed, 1)

            def scale_tables(it, h):
                pool.wait_ge(tables_loaded.sem, tables_loaded.past(it, ("load_tables", h)))
                for which in (QUERY, KEY):
                    last = nc.gpsimd.tensor_tensor(tables[:, which], tables[:, which],
                                                   scale_rows[:, which].unsqueeze(2).broadcast_to([P, 2, TILES, DH]), ALU.mult)
                last.then_inc(tables_ready.sem, 1)

            def norms(it, a):
                pool.wait_ge(clamped.sem, clamped.past(it, ("project_qk", a)))
                n = norm[:, a % TILES].rearrange("p i h -> p (i h)")
                nc.gpsimd.tensor_tensor(n, n, minus_half[:], ALU.pow).then_inc(norm_ready.sem, 1)

            def rope(it, a):
                pool.wait_ge(sin_ready.sem, sin_ready.past(it, ("rope", a)))
                for which in (QUERY, KEY):
                    last = nc.gpsimd.tensor_tensor(by_head(qk_tok[:, a % TILES])[:, which], by_head(qk_tok[:, a % TILES])[:, which],
                                                   table(COS, a % TILES)[:, which], ALU.mult)
                last.then_inc(cos_ready.sem, 1)

            pool.wait_ge(scales_loaded, 16 * SCALES)
            for kind, a in before:
                if kind == "scale_tables":
                    scale_tables(None, a)
                elif kind == "project_qk":
                    norms(None, a)
                elif kind == "rope":
                    rope(None, a)
            pool.wait_ge(consts_loaded, 16 * CONSTS)
            with pool.Fori(0, BATCH) as it:
                for kind, a in steps:
                    if kind == "weigh":
                        for head in (0, 1):
                            pool.wait_ge(weighed.sem, weighed.past(it, (kind, a), head))
                            part = prob[:, a % 2, head]
                            nc.gpsimd.tensor_tensor(part, part, weight[:, a % 2, head].unsqueeze(2).broadcast_to([P, 2, 2 * P]),
                                                    ALU.mult).then_inc(normalized.sem, 1)
                    elif kind == "scale_tables":
                        scale_tables(it, a)
                    elif kind == "project_qk":
                        norms(it, a)
                    elif kind == "rope":
                        rope(it, a)
                    elif kind == "ln_stats":
                        pool.wait_ge(var_ready.sem, var_ready.past(it, (kind, a)))
                        r = rstd[:, 2 * (a % 2):2 * (a % 2) + 2]
                        nc.gpsimd.tensor_tensor(r, r, minus_half[:, 0:2], ALU.pow).then_inc(rstd_ready.sem, 1)
                    elif kind == "x1_bias":
                        pool.wait_ge(ln_scaled.sem, ln_scaled.past(it, ("ln_apply", 2 * a + 1)))
                        if a == 0:
                            pool.wait_ge(edge_kept.sem, edge_kept.past(it, ("shift_keys", 0)))
                        nc.gpsimd.tensor_tensor(x1[:], x1[:], b2_row[:].unsqueeze(1).broadcast_to([P, TILES, D]), ALU.add).then_inc(x1_biased.sem, 1)
                    elif kind == "add_attended":
                        pool.wait_ge(attended_loaded.sem, attended_loaded.past(it, (kind, a)))
                        pool.wait_ge(x1_biased.sem, x1_biased.past(it, ("x1_bias", a)))
                        nc.gpsimd.tensor_tensor(x1[:], x1[:], x_tok[:], ALU.add).then_inc(attended_added.sem, 1)

        @block.tensor
        def _(pe):
            def take_bank(it, n):
                if n >= 3 or it is not None:
                    pe.wait_ge(emptied.sem, emptied.upto(it, n - 3 if n >= 3 else -1))
                return bank[n % 3]

            def products(out, lhs, rhs, tiles):
                order = [(c, a, b) for c in range(tiles) for a, b in PASSES]
                for i, (c, a, b) in enumerate(order):
                    last = nc.tensor.matmul(out, lhs(c, a), rhs(c, b), start=(i == 0), stop=(i == len(order) - 1))
                return last

            def transpose_tok(it, kind, h, source):
                for c in range(CT):
                    out = take_bank(it, filled.number(it, (kind, h), c))
                    for t in range(TILES):
                        last = nc.tensor.transpose(out[:, t * P:(t + 1) * P], source[:, t, c * P:(c + 1) * P], ident[:])
                    last.then_inc(filled.sem, 1)

            def prepare(it, kind, a):
                if kind == "transpose_x":
                    pe.wait_ge(x_loaded.sem, x_loaded.past(it, ("load_x", a)))
                    transpose_tok(it, kind, a, x_tok)
                elif kind == "project_qk":
                    if a % TILES == 0:
                        pe.wait_ge(emptied.sem, emptied.past(it, ("transpose_x", a // TILES), CT - 1))
                    for which in (QUERY, KEY):
                        out = take_bank(it, filled.number(it, (kind, a), which))
                        t = a % TILES
                        products(out[:], lambda c, part: actT[:, part, c, t * P:(t + 1) * P],
                                 lambda c, part: wqkv[:, part, c, which * F_INNER:(which + 1) * F_INNER], CT).then_inc(filled.sem, 1)
                elif kind == "project_v":
                    for t in range(TILES):
                        out = take_bank(it, filled.number(it, (kind, a), t))
                        products(out[:], lambda c, part: actT[:, part, c, t * P:(t + 1) * P],
                                 lambda c, part: wqkv[:, part, c, 2 * F_INNER:3 * F_INNER], CT).then_inc(filled.sem, 1)
                elif kind == "transpose_qk":
                    pe.wait_ge(roped.sem, roped.past(it, ("rope_sum", a)))
                    for which in (QUERY, KEY):
                        out = take_bank(it, filled.number(it, (kind, a), which))
                        for pair in range(PAIRS):
                            last = nc.tensor.transpose(out[:, pair * P:(pair + 1) * P], qk_tok[:, a % TILES, which, pair * P:(pair + 1) * P], ident[:])
                        last.then_inc(filled.sem, 1)

            pe.wait_ge(ident_loaded, 16)
            for kind, a in before:
                if kind == "project_qk" and a % TILES == 0:
                    pe.wait_ge(stage_emptied, 4)
                prepare(None, kind, a)
            pe.wait_ge(stage_emptied, len(pieces))
            pe.wait_ge(zeroed, 1)
            with pe.Fori(0, BATCH) as it:
                for kind, a in steps:
                    prepare(it, kind, a)
                    if kind == "scores":
                        half, s = divmod(a, UNITS)
                        pair, tile = s // 2, 2 * (s % 2)
                        if s == 0:
                            pe.wait_ge(emptied.sem, emptied.past(it, ("transpose_qk", half * TILES - 1), 1) if half else emptied.upto(it, -1))
                            if half:
                                pe.wait_ge(keys_shifted.sem, keys_shifted.past(it, ("shift_keys", 0)))
                        elif s == 1:
                            pe.wait_ge(x2_ready.sem, x2_ready.upto(it, 2 * half - 1))
                        pe.wait_ge(exped.sem, exped.past(it, ("scores", a - 2), 1) if a >= 2 else exped.upto(it, -1))
                        for t in (0, 1):
                            col = (tile + t) * P
                            for i, (qp, kp) in enumerate(PASSES):
                                for head in (0, 1):
                                    rows = slice(DH * head, DH * (head + 1))
                                    mm = nc.tensor.matmul(scores[a % 2][head][:, t, :], q_o[rows, qp, pair, col:col + P],
                                                          kT[rows, kp, pair, col:col + 2 * P], start=(i == 0), stop=(i == 2))
                        mm.then_inc(scored.sem, 1)
                    elif kind == "transpose":
                        for head in (0, 1):
                            out = take_bank(it, filled.number(it, (kind, a), head))
                            pe.wait_ge(normalized.sem, normalized.past(it, ("weigh", a), head))
                            for j in range(4):
                                last = nc.tensor.transpose(out[:, j * P:(j + 1) * P], prob[:, a % 2, head, j // 2, (j % 2) * P:(j % 2 + 1) * P],
                                                           ident[:])
                            last.then_inc(filled.sem, 1)
                    elif kind == "values":
                        half, pair = divmod(a, PAIRS)
                        pe.wait_ge(emptied.sem, emptied.past(it, ("transpose", 2 * a + 1), 1))
                        pe.wait_ge(o_emptied.sem, o_emptied.upto(it, a - 1))
                        order = [(kt, head, vp, pp) for kt in key_tiles(half) for head in (0, 1) for vp, pp in PASSES]
                        for i, ((tile, p0, p1, o0, o1), head, vp, pp) in enumerate(order):
                            mm = nc.tensor.matmul(o_bank[:, o0:o1], value_operand(half, tile, vp, pair, head),
                                                  probT[:, pp, head, p0:p1], start=(i == 0), stop=(i == len(order) - 1),
                                                  skip_group_check=True)
                        mm.then_inc(o_filled.sem, 1)
                    elif kind == "project_o":
                        pe.wait_ge(o_emptied.sem, o_emptied.past(it, ("values", PAIRS * (a + 1) - 1)))
                        for t in range(TILES):
                            out = take_bank(it, filled.number(it, (kind, a), t))
                            products(out[:, 0:D], lambda c, part: q_o[:, part, c, t * P:(t + 1) * P],
                                     lambda c, part: wo[:, part, c, :], PAIRS).then_inc(filled.sem, 1)
                    elif kind == "transpose_h":
                        pe.wait_ge(ln_ready.sem, ln_ready.past(it, ("ln_apply", 2 * a + 1)))
                        transpose_tok(it, kind, a, x_tok)
                    elif kind == "up":
                        j, m = hidden_of(a)
                        if j == 0:
                            pe.wait_ge(emptied.sem, emptied.past(it, ("transpose_h", a // FH), CT - 1))
                        for i, c0 in enumerate((HID, 0)):
                            out = take_bank(it, filled.number(it, (kind, a), i))
                            col = c0 + j * HT
                            products(out[0:m, :], lambda c, part: w1[:, part, c, col:col + m], lambda c, part: actT[:, part, c, :],
                                     CT).then_inc(filled.sem, 1)
                    elif kind == "down":
                        j, m = hidden_of(a)
                        pe.wait_ge(u_ready.sem, u_ready.past(it, ("up", a)))
                        if j == 0:
                            pe.wait_ge(exped.sem, exped.past(it, ("scores", (a // FH + 1) * UNITS - 1), 1))
                        for t in range(TILES):
                            for i, (up, wp) in enumerate(PASSES):
                                mm = nc.tensor.matmul(y_banks[t // 2][:, t % 2, :], u[0:m, a % 4, up, t * P:(t + 1) * P], w2[0:m, wp, j, :],
                                                      start=(j == 0 and t % 2 == 0 and i == 0), stop=(j == FH - 1 and t % 2 == 1 and i == 2),
                                                      skip_group_check=True)
                        mm.then_inc(downed.sem, 1)

        @block.scalar
        def _(act):
            act.sem_inc(exped.sem, 1)

            def take_high(it, kind, a):
                for i, place in enumerate(places_of(kind, a)):
                    n = filled.number(it, (kind, a), i)
                    act.wait_ge(filled.sem, filled.upto(it, n))
                    nc.scalar.activation(place(HI), like(bank[n % 3], place(HI)), ACT.Copy).then_inc(hi_taken.sem, 1)

            def take_raw(it, a):
                first = filled.number(it, ("project_qk", a))
                if it is not None and a >= TILES:
                    act.wait_ge(filled.sem, filled.past(it, ("transpose_qk", a - TILES), 1))
                elif it is not None:
                    act.wait_ge(filled.sem, filled.upto(it, -1))
                for which in (QUERY, KEY):
                    act.wait_ge(filled.sem, filled.upto(it, first + which))
                    nc.scalar.activation(qk_tok[:, a % TILES, which, :], bank[(first + which) % 3][:], ACT.Copy)
                    if ("project_qk", a - 1) in (emptied.first0 if it is None else emptied.first):
                        act.wait_ge(emptied.sem, emptied.past(it, ("project_qk", a - 1), which))
                    elif it is not None:
                        act.wait_ge(emptied.sem, emptied.upto(it, -1))
                    nc.scalar.activation(square[:, which, :], bank[(first + which) % 3][:], ACT.Square).then_inc(raw_taken.sem, 1)

            for kind, a in before:
                if kind == "split":
                    act.wait_ge(staged[a % 3], 16 * (a // 3 + 1))
                    nc.scalar.activation(pieces[a][1], stage_of(a), ACT.Copy).then_inc(stage_hi_taken, 1)
                elif kind in highs:
                    take_high(None, kind, a)
                elif kind == "project_qk":
                    take_raw(None, a)
            with act.Fori(0, BATCH) as it:
                for kind, a in steps:
                    if kind == "transpose_qk" and a == TILES - 1:
                        act.wait_ge(keys_shifted.sem, keys_shifted.past(it, ("shift_keys", 0)))
                    if kind in highs:
                        take_high(it, kind, a)
                    elif kind == "project_qk":
                        take_raw(it, a)
                    elif kind == "softmax":
                        for head in (0, 1):
                            act.wait_ge(negated.sem, negated.past(it, ("scores", a), head))
                            for t in (0, 1):
                                last = nc.scalar.activation(prob[:, a % 2, head, t, :], scores[a % 2][head][:, t, :], ACT.Exp,
                                                            bias=neg_max[:, a % 2, head, t:t + 1], accum_out=row_sum[:, a % 2, head, t:t + 1])
                            last.then_inc(exped.sem, 1)
                    elif kind == "values":
                        act.wait_ge(o_filled.sem, o_filled.past(it, (kind, a)))
                        nc.scalar.activation(q_o[:, HI, a % PAIRS, :], o_bank[:], ACT.Copy).then_inc(o_hi_taken.sem, 1)
                    elif kind == "up":
                        j, m = hidden_of(a)
                        n = filled.number(it, (kind, a), 0)
                        act.wait_ge(filled.sem, filled.upto(it, n))
                        if a >= 2:
                            act.wait_ge(u_ready.sem, u_ready.past(it, ("up", a - 2)))
                        nc.scalar.activation(gu[0:m, a % 2, :], bank[n % 3][0:m, :], ACT.Gelu, bias=b1_cols[0:m, 1, j:j + 1]).then_inc(gelued.sem, 1)
                        act.wait_ge(emptied.sem, emptied.past(it, (kind, a), 1))
                        if j >= 4:
                            act.wait_ge(downed.sem, downed.past(it, ("down", a - 4)))
                        nc.scalar.activation(u[0:m, a % 4, HI, :], gu[0:m, a % 2, :], ACT.Copy).then_inc(u_hi.sem, 1)

        @block.vector
        def _(dve):
            dve.sem_inc(o_emptied.sem, 1)
            dve.sem_inc(x2_ready.sem, 1)

            def take_low(it, kind, a):
                for i, place in enumerate(places_of(kind, a)):
                    n = filled.number(it, (kind, a), i)
                    dve.wait_ge(hi_taken.sem, hi_taken.past(it, (kind, a), i))
                    nc.vector.tensor_tensor(place(LO), like(bank[n % 3], place(LO)), place(HI).bitcast(F32), ALU.subtract).then_inc(emptied.sem, 1)

            def sum_squares(it, a):
                for which in (QUERY, KEY):
                    dve.wait_ge(raw_taken.sem, raw_taken.past(it, ("project_qk", a), which))
                    nc.vector.tensor_reduce(norm[:, a % TILES, which, :], square[:, which, :].rearrange("p (h d) -> p h d", d=DH), AXIS.X,
                                            ALU.add).then_inc(emptied.sem, 1)
                dve.wait_ge(emptied.sem, emptied.past(it, ("project_qk", a), KEY))
                nc.vector.tensor_scalar(norm[:, a % TILES], norm[:, a % TILES], 1e-24, None, ALU.max).then_inc(clamped.sem, 1)

            def rope(it, a):
                if a % TILES == 0:
                    dve.wait_ge(tables_ready.sem, tables_ready.past(it, ("scale_tables", a // TILES)))
                raw, sin, lower, upper = by_head(qk_tok[:, a % TILES]), table(SIN, a % TILES), slice(0, DH // 2), slice(DH // 2, DH)
                nc.vector.tensor_tensor(by_head(sin_part[:])[:, :, :, lower], raw[:, :, :, upper], sin[:, :, :, lower], ALU.mult)
                nc.vector.tensor_tensor(by_head(sin_part[:])[:, :, :, upper], raw[:, :, :, lower], sin[:, :, :, upper],
                                        ALU.mult).then_inc(sin_ready.sem, 1)

            def rope_sum(it, a):
                place = qk_tok[:, a % TILES]
                dve.wait_ge(cos_ready.sem, cos_ready.past(it, ("rope", a)))
                nc.vector.tensor_tensor(place, place, sin_part[:], ALU.add).then_inc(rope_added.sem, 1)
                dve.wait_ge(norm_ready.sem, norm_ready.past(it, ("project_qk", a)))
                dve.wait_ge(rope_added.sem, rope_added.past(it, ("rope_sum", a)))
                nc.vector.tensor_tensor(by_head(place), by_head(place), norm[:, a % TILES].unsqueeze(3).broadcast_to([P, 2, F_HEADS, DH]),
                                        ALU.mult).then_inc(roped.sem, 1)

            for kind, a in before:
                if kind == "split":
                    _, hi, lo = pieces[a]
                    dve.wait_ge(stage_hi_taken, a + 1)
                    nc.vector.tensor_tensor(lo, stage_of(a), hi.bitcast(F32), ALU.subtract).then_inc(stage_emptied, 1)
                elif kind in highs:
                    take_low(None, kind, a)
                elif kind == "project_qk":
                    sum_squares(None, a)
                elif kind == "rope":
                    rope(None, a)
                elif kind == "rope_sum":
                    rope_sum(None, a)
            dve.wait_ge(consts_loaded, 16 * CONSTS)
            with dve.Fori(0, BATCH) as it:
                for kind, a in steps:
                    if kind == "scores":
                        half, s = divmod(a, UNITS)
                        tile = 2 * (s % 2)
                        dve.wait_ge(scored.sem, scored.past(it, (kind, a)))
                        dve.sem_inc(dve_carried, 1)
                        for head in (0, 1):
                            for t in (0, 1):
                                sc = scores[a % 2][head][:, t, :]
                                last = nc.vector.tensor_tensor_reduce(out=sc, in0=sc, in1=mask[:, min(half * TILES + tile + t, 1)], scale=1.0,
                                                                      scalar=-3e38, op0=ALU.add, op1=ALU.max,
                                                                      accum_out=row_max[:, a % 2, head, t:t + 1])
                            last.then_inc(maxed.sem, 1)
                            dve.wait_ge(maxed.sem, maxed.past(it, (kind, a), head))
                            nc.vector.tensor_scalar(neg_max[:, a % 2, head], row_max[:, a % 2, head], -1.0, None, ALU.mult).then_inc(negated.sem, 1)
                    elif kind in highs:
                        take_low(it, kind, a)
                    elif kind == "weigh":
                        for head in (0, 1):
                            dve.wait_ge(exped.sem, exped.past(it, ("scores", a), head))
                            nc.vector.reciprocal(weight[:, a % 2, head], row_sum[:, a % 2, head]).then_inc(weighed.sem, 1)
                    elif kind == "values":
                        dve.wait_ge(o_hi_taken.sem, o_hi_taken.past(it, (kind, a)))
                        nc.vector.tensor_tensor(q_o[:, LO, a % PAIRS, :], o_bank[:], q_o[:, HI, a % PAIRS, :].bitcast(F32),
                                                ALU.subtract).then_inc(o_emptied.sem, 1)
                    elif kind == "project_qk":
                        sum_squares(it, a)
                    elif kind == "rope":
                        rope(it, a)
                    elif kind == "rope_sum":
                        rope_sum(it, a)
                    elif kind == "project_o":
                        dve.wait_ge(x1_loaded.sem, x1_loaded.past(it, ("load_x1", a)))
                        for t in range(TILES):
                            n = filled.number(it, (kind, a), t)
                            dve.wait_ge(filled.sem, filled.upto(it, n))
                            nc.vector.tensor_tensor(x1[:, t, :], bank[n % 3][:, 0:D], x1[:, t, :], ALU.add).then_inc(emptied.sem, 1)
                    elif kind == "ln_stats":
                        dve.wait_ge(emptied.sem, emptied.past(it, ("project_o", a // 2), 2 * (a % 2) + 1))
                        half_shifted = shifted[a % 2]
                        dve.wait_ge(half_shifted.sem, half_shifted.past(it, ("shift_back" if a % 2 else "shift_front", a // 2)))
                        for t in (2 * (a % 2), 2 * (a % 2) + 1):
                            nc.vector.bn_stats(bn[:, t, 0, :], x1[:, t, 0:P])
                            last = nc.vector.bn_stats(bn[:, t, 1, :], x_tok[:, t, P:D])
                        last.then_inc(bn_done.sem, 1)
                        dve.wait_ge(bn_done.sem, bn_done.past(it, (kind, a)))
                        dve.sem_inc(dve_carried, 1)
                        for t in (2 * (a % 2), 2 * (a % 2) + 1):
                            last = nc.vector.bn_aggr(mean_var[:, t, :], bn[:, t])
                        last.then_inc(aggregated.sem, 1)
                        dve.wait_ge(aggregated.sem, aggregated.past(it, (kind, a)))
                        two = slice(2 * (a % 2), 2 * (a % 2) + 2)
                        nc.vector.tensor_scalar(rstd[:, two], mean_var[:, two, 1], 1e-5, None, ALU.add).then_inc(var_ready.sem, 1)
                    elif kind == "ln_apply":
                        for t in (2 * (a % 2), 2 * (a % 2) + 1):
                            for source, cols in ((x1, slice(0, P)), (x_tok, slice(P, D))):
                                last = nc.vector.scalar_tensor_tensor(out=x_tok[:, t, cols], in0=source[:, t, cols], scalar=mean_var[:, t, 0:1],
                                                                      in1=ln_g_row[:, cols], op0=ALU.subtract, op1=ALU.mult)
                        last.then_inc(ln_scaled.sem, 1)
                        dve.wait_ge(ln_scaled.sem, ln_scaled.past(it, (kind, a)))
                        dve.wait_ge(rstd_ready.sem, rstd_ready.past(it, ("ln_stats", a)))
                        for t in (2 * (a % 2), 2 * (a % 2) + 1):
                            last = nc.vector.scalar_tensor_tensor(out=x_tok[:, t, :], in0=x_tok[:, t, :], scalar=rstd[:, t:t + 1], in1=ln_b_row[:],
                                                                  op0=ALU.mult, op1=ALU.add)
                        last.then_inc(ln_ready.sem, 1)
                    elif kind == "up":
                        j, m = hidden_of(a)
                        dve.wait_ge(gelued.sem, gelued.past(it, (kind, a)))
                        n = filled.number(it, (kind, a), 1)
                        dve.wait_ge(filled.sem, filled.upto(it, n))
                        nc.vector.scalar_tensor_tensor(out=gu[0:m, a % 2, :], in0=bank[n % 3][0:m, :], scalar=b1_cols[0:m, 0, j:j + 1],
                                                       in1=gu[0:m, a % 2, :], op0=ALU.add, op1=ALU.mult).then_inc(emptied.sem, 2)
                        dve.wait_ge(u_hi.sem, u_hi.past(it, (kind, a)))
                        nc.vector.tensor_tensor(u[0:m, a % 4, LO, :], gu[0:m, a % 2, :], u[0:m, a % 4, HI, :].bitcast(F32),
                                                ALU.subtract).then_inc(u_ready.sem, 1)
                    elif kind == "out":
                        last_step = ("add_attended", a) if attended is not None else ("x1_bias", a)
                        done = attended_added if attended is not None else x1_biased
                        dve.wait_ge(downed.sem, downed.past(it, ("down", (a + 1) * FH - 1)))
                        dve.wait_ge(done.sem, done.past(it, last_step))
                        for i in (0, 1):
                            nc.vector.tensor_tensor(x1[:, 2 * i:2 * i + 2, :], y_banks[i][:], x1[:, 2 * i:2 * i + 2, :],
                                                    ALU.add).then_inc(x2_ready.sem, 1)


def local_attention_program(nc, x, gamma, w_qkv, w_gates, b_gates, w_out, wqkv, q_scale, k_scale, wo, ln_g, ln_b, w1, b1, w2, b2,
                            gated_masks, layer_masks, identity, tables, out):
    normed = nc.dram_tensor("normed", [BATCH, SEQ + 1, D], F32).ap()
    hidden = nc.dram_tensor("hidden", [BATCH, SEQ + 1, D], F32).ap()
    attended = nc.dram_tensor("attended", [BATCH, SEQ, D], F32).ap()
    attention_phase(nc, x, gamma, w_qkv, w_gates, b_gates, w_out, gated_masks, identity, normed, hidden, attended)
    weights = (wqkv, q_scale, k_scale, wo, ln_g, ln_b, w1, b1, w2, b2)
    ffn_phase(nc, 0, normed, hidden, 1, None, *[w[0] for w in weights], layer_masks, identity, tables)
    ffn_phase(nc, 1, hidden, out, 0, attended, *[w[1] for w in weights], layer_masks, identity, tables)


def window_masks(window):
    query, key = np.arange(P)[:, None], np.arange(2 * P)[None]
    distance = P + query - key
    other = np.where((distance >= 0) & (distance <= window), 0.0, MASKED)
    first = np.where(key < P, MASKED, other)
    return np.stack([first, other]).astype(np.float32)


def rotary_tables():
    f = np.float32
    half_idx = np.arange(0, DH, 2, dtype=f)
    inv_freq = f(1) / f(10000) ** (half_idx / f(DH))
    t = np.arange(SEQ, dtype=f)
    freqs = t[:, None] * inv_freq[None, :]
    base = (half_idx + f(0.4 * DH)) / f(1.4 * DH)
    scale = base[None, :] ** ((t - SEQ // 2) / f(F_WINDOW // 2))[:, None]
    freqs, scale = (np.concatenate([a, a], axis=-1) for a in (freqs, scale))
    sign = np.where(np.arange(DH) < DH // 2, f(-1), f(1))
    cos, sin = np.cos(freqs), np.sin(freqs) * sign
    tables = np.stack([f(8) * cos * scale, f(8) * sin * scale, cos / scale, sin / scale], axis=1)
    return tables.reshape(HALVES, TILES, P, 2, 2, DH).transpose(0, 2, 3, 4, 1, 5).astype(f)


def kernel(L0_attn_x, L0_attn_gamma, L0_attn_W_qkv, L0_attn_W_gates, L0_attn_b_gates, L0_attn_W_out, L0_ffn_wqkv, L0_ffn_q_scale,
           L0_ffn_k_scale, L0_ffn_wo, L0_ffn_ln_g, L0_ffn_ln_b, L0_ffn_w1, L0_ffn_b1, L0_ffn_w2, L0_ffn_b2):
    import concourse.bacc as bacc
    from concourse.bass_utils import run_bass_kernel_spmd

    arrays = {
        "x": L0_attn_x, "gamma": L0_attn_gamma, "w_qkv": L0_attn_W_qkv, "w_gates": L0_attn_W_gates, "b_gates": L0_attn_b_gates,
        "w_out": L0_attn_W_out, "wqkv": L0_ffn_wqkv, "q_scale": L0_ffn_q_scale, "k_scale": L0_ffn_k_scale, "wo": L0_ffn_wo,
        "ln_g": L0_ffn_ln_g, "ln_b": L0_ffn_ln_b, "w1": L0_ffn_w1, "b1": L0_ffn_b1, "w2": L0_ffn_w2, "b2": L0_ffn_b2,
        "gated_masks": window_masks(A_WINDOW), "layer_masks": window_masks(F_WINDOW), "identity": np.eye(P, dtype=np.float32),
        "tables": rotary_tables()}
    arrays = {f"in_{name}": np.ascontiguousarray(a) for name, a in arrays.items()}
    nc = bacc.Bacc("TRN2", target_bir_lowering=False, num_devices=1)
    args = [nc.dram_tensor(name, a.shape, mybir.dt.from_np(a.dtype), kind="ExternalInput").ap() for name, a in arrays.items()]
    out = nc.dram_tensor("out", (BATCH, SEQ, D), F32, kind="ExternalOutput").ap()
    local_attention_program(nc, *args, out)
    return run_bass_kernel_spmd(nc, [arrays], core_ids=[0]).results[0]["out"]
```
